# Optimizing a Trainium2 kernel written in Bass

```python
import numpy as np
import jax
import jax.numpy as jnp

def _softmax(x, axis=-1):
    return jax.nn.softmax(x, axis=axis)

def _gelu(x):
    return jax.nn.gelu(x, approximate=True)

def _silu(x):
    return jax.nn.silu(x)

def _sigmoid(x):
    return jax.nn.sigmoid(x)

def _layernorm(x, axis=-1, eps=1e-05):
    m = jnp.mean(x, axis=axis, keepdims=True)
    v = jnp.var(x, axis=axis, keepdims=True)
    return (x - m) / jnp.sqrt(v + eps)

def _scatter_add(tgt, idx, src, axis=0):
    return tgt.at[idx].add(src)

def _segment_sum(src, seg, n):
    return jax.ops.segment_sum(src, seg, n)
kernel_name = 'mk_adj_preln_d1_adj_r2_3d3795'

def setup_inputs(seed: int=0):
    np.random.seed(seed)
    _w = jnp.asarray

    def _rec_inputs():
        import jax
        import jax.numpy as jnp
        _gk = jax.random.key(seed)
        x = -1.394e-06 + 0.9999 * jax.random.normal(jax.random.fold_in(_gk, 1), (8192, 256), jnp.float32)
        _a = jax.random.bernoulli(jax.random.fold_in(_gk, 2), 0.000488281, (8192, 8192))
        _a = jnp.logical_or(_a, jnp.swapaxes(_a, -1, -2))
        _a = jnp.logical_or(_a, jnp.eye(8192, dtype=bool))
        adj = _a.astype(jnp.int32)
        return (x, adj)
    x, adj = _rec_inputs()

    def _L0_gnn_setup():
        import jax, jax.numpy as jnp
        import numpy as np
        N = 4096
        IN_F = 256
        OUT_F = 256
        ALPHA = 0.2
        NEG_BIG = -9000000000000000.0
        key = jax.random.key(seed)
        k1, k2, k3, k4 = jax.random.split(key, 4)
        adjacency = jax.random.randint(k1, (N, N), 0, 2, dtype=jnp.int32)
        features = jax.random.normal(k2, (N, IN_F), dtype=jnp.float32)
        W = jax.random.normal(k3, (IN_F, OUT_F), dtype=jnp.float32) * (1.0 / np.sqrt(IN_F))
        attn = jax.random.normal(k4, (2 * OUT_F, 1), dtype=jnp.float32) * 0.05
        return {'adjacency': adjacency, 'features': features, 'W': W, 'attn': attn}
    _L0_gnn_all = _L0_gnn_setup()
    _L0_gnn_in = {k: v for k, v in _L0_gnn_all.items() if k in ('W', 'attn')}
    del _L0_gnn_all
    return {'x': x, 'adj': adj, 'L0_gnn_W': _L0_gnn_in['W'], 'L0_gnn_attn': _L0_gnn_in['attn']}

def reference(x, adj, L0_gnn_W, L0_gnn_attn):
    import jax
    import jax.numpy as jnp

    def _L0_gnn_ref(adjacency, features, W, attn):
        import jax, jax.numpy as jnp
        import numpy as np
        N = 4096
        IN_F = 256
        OUT_F = 256
        ALPHA = 0.2
        NEG_BIG = -9000000000000000.0
        h = features @ W
        a1 = attn[:OUT_F, 0]
        a2 = attn[OUT_F:, 0]
        s1 = h @ a1
        s2 = h @ a2
        e = jax.nn.leaky_relu(s1[:, None] + s2[None, :], negative_slope=ALPHA)
        e = jnp.where(adjacency > 0, e, NEG_BIG)
        attention = jax.nn.softmax(e, axis=1)
        h_prime = attention @ h
        return jax.nn.elu(h_prime)
    h = jnp.maximum(_layernorm(x, axis=-1), 0.0)
    x = x + _L0_gnn_ref(adj, h, L0_gnn_W, L0_gnn_attn)
    return x

_drawn_inputs = setup_inputs


def setup_inputs(seed=0):
    import zlib

    import numpy as np

    out = dict(_drawn_inputs(seed))
    spreads = {}
    factors = {}
    for name, (base, spread) in spreads.items():
        noise = np.random.default_rng([zlib.crc32(name.encode()), seed]).standard_normal(out[name].shape)
        drawn = base * np.exp(spread * noise) if base else spread * noise
        out[name] = jnp.asarray(drawn.astype(out[name].dtype))
    for name, factor in factors.items():
        out[name] = (out[name] * factor).astype(out[name].dtype)
    return out
```

```python
import concourse.bass as bass
from concourse import mybir
from contextlib import ExitStack
import math

FP32 = mybir.dt.float32
FP16 = mybir.dt.float16
BF16 = mybir.dt.bfloat16
I32 = mybir.dt.int32
ALU = mybir.AluOpType
ACT = mybir.ActivationFunctionType
AX = mybir.AxisListType

PART = 128
SLOPE = 0.2
LN_EPS = 1e-5
VALUE_SCALE = 256.0
WEIGHT_SCALE = 64.0
RSQRT_SEED = float(0x5F3759DF)
NEWTON_STEPS = 3


def gat_kernel(nc, x, adj, W, attn, out):
    N, F = x.shape
    O = W.shape[1]
    TILES = N // PART
    GROUP = 8
    GROUPS = TILES // GROUP
    KC = F // PART
    HC = O + 2
    CHUNK = 2048
    CHUNKS = N // CHUNK
    STAGE = 1024
    STAGES = N // STAGE
    BLOCKS = STAGE // PART
    PSLOTS = 3
    VALUE_STEPS = 4
    SPLITS = 4

    x_groups = x.rearrange("(t p) f -> p t f", p=PART)
    out_rows = out
    attn_rows = attn.rearrange("(two n) one -> one two n", two=2)

    u_dram = nc.dram_tensor("u_row", [TILES, PART], FP32).ap()

    ctx = ExitStack()
    with ctx:
        def sb(name, shape, dt):
            return ctx.enter_context(nc.sbuf_tensor(name, shape, dt))

        def sem(name):
            return ctx.enter_context(nc.semaphore(name))

        ident = sb("ident", [PART, PART], FP32)
        ones = sb("ones", [PART, PART], FP32)
        w_ext = sb("w_ext", [PART, KC, HC], FP32)
        attn_bc = sb("attn_bc", [PART, 2, O], FP32)
        scratch = sb("scratch", [PART, O], FP32)
        stats = sb("stats", [PART, GROUP, 6], FP32)
        mean_var = sb("mean_var", [PART, GROUP, 2], FP32)
        var_eps = sb("var_eps", [PART, GROUP], FP32)
        seed = sb("seed", [PART, GROUP], I32)
        rstd = sb("rstd", [PART, 2, GROUP], FP32)
        newton = sb("newton", [PART, GROUP], FP32)
        shift = sb("shift", [PART, 2, GROUP], FP32)
        feat = sb("feat", [PART, 4, F], FP32)
        featT = sb("featT", [PART, 2, KC, PART], FP32)
        d_col = sb("d_col", [PART, 2, GROUP], FP32)
        d_scaled = sb("d_scaled", [PART, GROUP], FP32)
        s_all = sb("s_all", [PART, 2, TILES], FP32)
        r_all = sb("r_all", [PART, TILES], FP32)
        h_mean = sb("h_mean", [PART, O], FP32)
        ext = sb("ext", [PART, 3], FP32)
        row_max = sb("row_max", [3, 1], FP32)
        row_diag = sb("row_diag", [3, 3], FP32)
        u_bias = sb("u_bias", [PART, 1], FP32)
        uT = sb("uT", [TILES, PART], FP32)

        value_hi = sb("value_hi", [PART, TILES, O + 2], FP16)
        value_lo = sb("value_lo", [PART, TILES, O], FP16)
        u_bc = sb("u_bc", [PART, N], FP32)
        adj_in = sb("adj_in", [PART, CHUNKS, CHUNK], I32)
        mask = sb("mask", [PART, 2, CHUNK], BF16)
        p_buf = sb("p_buf", [PART, 2, CHUNK + 16], FP32)
        pT_hi = sb("pT_hi", [PART, SPLITS, STAGE], FP16)
        pT_lo = sb("pT_lo", [PART, SPLITS, STAGE], FP16)
        r_cur = sb("r_cur", [PART, 2], FP32)
        x_tile = sb("x_tile", [PART, 2, F], FP32)
        y = sb("y", [PART, O], FP32)
        mean_part = sb("mean_part", [PART, O], FP32)
        neg_part = sb("neg_part", [PART, O], FP32)
        expm = sb("expm", [PART, O], FP32)
        x_plus = sb("x_plus", [PART, O], FP32)
        o_tile = sb("o_tile", [PART, 2, O], FP32)
        den = sb("den", [PART, 4], FP32)

        x_in = u_bc[:, 0:2 * GROUP * F].rearrange("p (b t f) -> p b t f", b=2, t=GROUP)
        scaled_h = u_bc[:, 2 * GROUP * F:3 * GROUP * F].rearrange("p (t f) -> p t f", t=GROUP)
        h_sum = u_bc[:, 3 * GROUP * F:4 * GROUP * F].rearrange("p (t f) -> p t f", t=GROUP)
        h_buf = p_buf[:, :, :].rearrange("p b (t f) -> p b t f", t=GROUP)

        ps_t = [ctx.enter_context(nc.psum_tensor(f"ps_t{i}", [PART, STAGE], FP32)) for i in range(PSLOTS)]
        acc = [ctx.enter_context(nc.psum_tensor(f"acc{i}", [PART, 512], FP32)) for i in range(2)]
        ps_feat = [ps_t[0][:, 0:F], ps_t[1][:, 0:F]]
        ps_h = [ps_t[0][:, 512:512 + HC], ps_t[1][:, 512:512 + HC]]
        ps_small = ps_t[2]

        w_loaded = sem("w_loaded")
        const_ready = sem("const_ready")
        wa_step = sem("wa_step")
        x_loaded = [sem("x_loaded0"), sem("x_loaded1")]
        norm_step = sem("norm_step")
        norm_ready = sem("norm_ready")
        feat_ready = sem("feat_ready")
        featT_done = sem("featT_done")
        featT_ready = sem("featT_ready")
        h_done = sem("h_done")
        h_ready = sem("h_ready")
        d_ready = sem("d_ready")
        value_step = sem("value_step")
        scaled_ready = sem("scaled_ready")
        hi_cut = sem("hi_cut")
        lo_cut = sem("lo_cut")
        h_summed = sem("h_summed")
        ext_ready = sem("ext_ready")
        ext_step = sem("ext_step")
        extT_done = sem("extT_done")
        s2T_done = sem("s2T_done")
        diag_ready = sem("diag_ready")
        glob_done = sem("glob_done")
        bias_ready = sem("bias_ready")
        uT_ready = sem("uT_ready")
        u_stored = sem("u_stored")
        u_loaded = [sem(f"u_loaded{c}") for c in range(CHUNKS)]
        r_ready = sem("r_ready")
        mean_done = sem("mean_done")
        mean_ready = sem("mean_ready")

        adj_loaded = [sem(f"adj_loaded{c}") for c in range(CHUNKS)]
        mask_ready = sem("mask_ready")
        r_picked = sem("r_picked")
        p_ready = sem("p_ready")
        pT_done = sem("pT_done")
        hi_ready = sem("hi_ready")
        lo_ready = sem("lo_ready")
        stage_summed = sem("stage_summed")
        epi_step = sem("epi_step")
        y_ready = sem("y_ready")
        neg_ready = sem("neg_ready")
        expm_ready = sem("expm_ready")
        xp_ready = sem("xp_ready")
        out_ready = sem("out_ready")
        x_back = [sem("x_back0"), sem("x_back1")]
        out_stored = [sem("out_stored0"), sem("out_stored1")]

        block = ctx.enter_context(nc.Block())

        PAIRS = TILES // 2

        def in_pairs(eng, pairs, pair):
            pair(0, True, False)
            with eng.Fori(1, pairs - 1) as k:
                pair(k, False, False)
            pair(pairs - 1, False, True)

        @block.sync
        def _(sync):
            for k in range(KC):
                sync.dma_start(w_ext[:, k, 0:O], W[k * PART:(k + 1) * PART, :]).then_inc(w_loaded, 16)
            sync.dma_start(attn_bc[:, :, :], attn_rows.to_broadcast([PART, 2, O])).then_inc(w_loaded, 16)

            def adj_chunk(t, c):
                sync.dma_start(adj_in[:, c, :], adj[bass.ts(t, PART), c * CHUNK:(c + 1) * CHUNK]) \
                    .then_inc(adj_loaded[c], 16)

            def load_groups(k, first):
                for b in range(2):
                    g = 2 * k + b
                    if not first:
                        sync.wait_ge(feat_ready, (g - 1) * GROUP)
                    sync.dma_start(x_in[:, b, :, :], x_groups[:, bass.ts(g, GROUP), :]) \
                        .then_inc(x_loaded[b], 16)

            load_groups(0, True)
            for c in range(CHUNKS):
                adj_chunk(0, c)
            with sync.Fori(1, GROUPS // 2) as k:
                load_groups(k, False)

            sync.wait_ge(uT_ready, 1)
            sync.dma_start(u_dram, uT[:, :]).then_inc(u_stored, 16)
            sync.wait_ge(u_stored, 16)
            sync.wait_ge(lo_cut, GROUPS)
            sync.wait_ge(mean_done, 1)
            u_rows = u_dram.rearrange("(one t) p -> one (t p)", one=1)
            for c in range(CHUNKS):
                part = slice(c * CHUNK, (c + 1) * CHUNK)
                sync.dma_start(u_bc[:, part], u_rows[:, part].to_broadcast([PART, CHUNK])) \
                    .then_inc(u_loaded[c], 16)

            def pair(k, first, last):
                for b in range(2):
                    t = 2 * k + b
                    if not first:
                        sync.wait_ge(xp_ready, t - 1)
                    sync.dma_start(x_tile[:, b, :], x[bass.ts(t, PART), :]).then_inc(x_back[b], 16)
                    if not (last and b == 1):
                        for c in range(CHUNKS):
                            sync.wait_ge(mask_ready, CHUNKS * t + c + 1)
                            adj_chunk(t + 1, c)
                    if not (first and b == 0):
                        sync.wait_ge(out_ready, t)
                        sync.dma_start(out_rows[bass.ts(t - 1, PART), :], o_tile[:, 1 - b, :]) \
                            .then_inc(out_stored[1 - b], 16)

            in_pairs(sync, PAIRS, pair)
            sync.wait_ge(out_ready, TILES)
            sync.dma_start(out_rows[(TILES - 1) * PART:TILES * PART, :], o_tile[:, 1, :]) \
                .then_inc(out_stored[1], 16)
            for b in range(2):
                sync.wait_ge(out_stored[b], 16 * PAIRS + 16)

        @block.gpsimd
        def _(pool):
            pool.memset(ones[:, :], 1.0).then_inc(const_ready, 1)
            pool.memset(ident[:, :], 0.0).then_inc(const_ready, 1)
            pool.wait_ge(const_ready, 2)
            pool.affine_select(out=ident[:, :], in_=ident[:, :], compare_op=ALU.not_equal, fill=1.0,
                               base=0, pattern=[[-1, PART]], channel_multiplier=1).then_inc(const_ready, 1)
            pool.memset(h_sum, 0.0).then_inc(h_summed, 1)
            for b in range(2):
                pool.memset(o_tile[:, b, :], 0.0).then_inc(out_stored[b], 16)

            def two_groups(k, first, last):
                for b in range(2):
                    g = 2 * k + b
                    pool.wait_ge(h_ready, (g + 1) * GROUP)
                    pool.wait_ge(h_summed, g + 1)
                    nc.gpsimd.tensor_tensor(h_sum, h_sum, h_buf[:, b, :, 0:O], ALU.add) \
                        .then_inc(h_summed, 1)

            in_pairs(pool, GROUPS // 2, two_groups)

        @block.scalar
        def _(act):
            LAG = 3

            def h_out(g, b, i, first):
                act.wait_ge(h_done, g * GROUP + i + 1)
                if i == 0 and not first:
                    act.wait_ge(scaled_ready, g - 1)
                    act.wait_ge(value_step, (g - 1) * VALUE_STEPS)
                    act.wait_ge(h_summed, g)
                nc.scalar.activation(h_buf[:, b, i, :], ps_h[i % 2], ACT.Copy).then_inc(h_ready, 1)

            def make_d(g, b):
                act.wait_ge(h_ready, (g + 1) * GROUP)
                nc.scalar.activation(d_col[:, b, :], h_buf[:, b, :, O + 1], ACT.Exp, scale=SLOPE) \
                    .then_inc(d_ready, 1)

            def cut_hi(g):
                act.wait_ge(scaled_ready, g + 1)
                nc.scalar.activation(value_hi[:, bass.ts(g, GROUP), 0:O], scaled_h, ACT.Copy) \
                    .then_inc(hi_cut, 1)

            def two_groups(k, first, last):
                for b in range(2):
                    g = 2 * k + b
                    start = first and b == 0
                    for i in range(GROUP):
                        if i == 0:
                            act.wait_ge(norm_ready, g + 1)
                        if not (start and i < 4):
                            act.wait_ge(featT_done, g * GROUP + i - 3)
                        nc.scalar.activation(feat[:, i % 4, :], x_in[:, b, i, :], ACT.Relu,
                                             bias=shift[:, b, i:i + 1], scale=rstd[:, b, i:i + 1]) \
                            .then_inc(feat_ready, 1)
                        if i >= LAG:
                            h_out(g, b, i - LAG, first)
                        elif not start:
                            h_out(g - 1, 1 - b, i - LAG + GROUP, first)
                        if i == LAG - 1 and not start:
                            make_d(g - 1, 1 - b)
                        if i == 6 and not start:
                            cut_hi(g - 1)
                    if last and b == 1:
                        for i in range(GROUP - LAG, GROUP):
                            h_out(g, b, i, first)
                        make_d(g, b)
                        cut_hi(g)

            def make_mask(t, c, start):
                act.wait_ge(adj_loaded[c], 16 * t + 16)
                if not start:
                    act.wait_ge(p_ready, CHUNKS * t + c - 1)
                nc.scalar.activation(mask[:, c % 2, :], adj_in[:, c, :], ACT.Sign).then_inc(mask_ready, 1)

            make_mask(0, 0, True)
            make_mask(0, 1, True)
            in_pairs(act, GROUPS // 2, two_groups)

            act.wait_ge(bias_ready, 1)
            act.wait_ge(s2T_done, 1)
            nc.scalar.activation(uT[:, :], ps_small[0:TILES, 256:256 + PART], ACT.Exp,
                                 bias=u_bias[0:TILES, 0:1], scale=1.0 - SLOPE).then_inc(uT_ready, 1)
            nc.scalar.activation(r_all[:, :], s_all[:, 0, :], ACT.Exp, bias=u_bias[:, 0:1],
                                 scale=SLOPE - 1.0).then_inc(r_ready, 1)
            act.wait_ge(mean_done, 1)
            nc.scalar.activation(h_mean[:, :], ps_small[:, 512:512 + O], ACT.Copy, scale=1.0 / N) \
                .then_inc(mean_ready, 1)

            def elu_exp(t):
                act.wait_ge(y_ready, t + 1)
                nc.scalar.activation(neg_part[:, :], y[:, :], ACT.Relu, scale=-1.0).then_inc(neg_ready, 1)
                act.wait_ge(neg_ready, t + 1)
                nc.scalar.activation(expm[:, :], neg_part[:, :], ACT.Exp, scale=-1.0) \
                    .then_inc(expm_ready, 1)

            def pair(k, first, last):
                for b in range(2):
                    t = 2 * k + b
                    for c in range(STAGES):
                        s = STAGES * t + c
                        act.wait_ge(pT_done, s + 1)
                        if not (first and b == 0 and c < SPLITS):
                            act.wait_ge(stage_summed, s - SPLITS + 1)
                        nc.scalar.activation(pT_hi[:, c % SPLITS, :], ps_t[c % PSLOTS][:, :], ACT.Relu) \
                            .then_inc(hi_ready, 1)
                        if c % 2 == 1:
                            if c < 4:
                                make_mask(t, c // 2 + 2, False)
                            elif not (last and b == 1):
                                make_mask(t + 1, c // 2 - 2, False)
                        if c == 4 and not (first and b == 0):
                            elu_exp(t - 1)

            in_pairs(act, PAIRS, pair)
            elu_exp(TILES - 1)

        @block.vector
        def _(dve):
            dve.wait_ge(w_loaded, 16 * (KC + 1))
            n = 0
            for k in range(KC):
                for a in range(2):
                    if n:
                        dve.wait_ge(wa_step, n)
                    nc.vector.scalar_tensor_tensor(out=scratch[:, :], in0=w_ext[:, k, 0:O], scalar=1.0,
                                                   in1=attn_bc[:, a, :], op0=ALU.mult, op1=ALU.mult,
                                                   accum_out=w_ext[:, k, O + a:O + a + 1]) \
                        .then_inc(wa_step, 1)
                    n += 1

            NORM = GROUP + 4 + 3 * NEWTON_STEPS

            def normalise(g, b, k, has_before):
                done = g * NORM
                dve.wait_ge(x_loaded[b], 16 * k + 16)
                for i in range(GROUP):
                    nc.vector.bn_stats(stats[:, i, :], x_in[:, b, i, :]).then_inc(norm_step, 1)
                dve.wait_ge(norm_step, done + GROUP)
                dve.nop(nofuse=True)
                for i in range(GROUP):
                    last = nc.vector.bn_aggr(mean_var[:, i, :], stats[:, i, :])
                last.then_inc(norm_step, 1)
                dve.wait_ge(norm_step, done + GROUP + 1)
                nc.vector.tensor_scalar(var_eps[:, :], mean_var[:, :, 1], LN_EPS, None, ALU.add) \
                    .then_inc(norm_step, 1)
                dve.wait_ge(norm_step, done + GROUP + 2)
                nc.vector.tensor_scalar(seed[:, :], var_eps[:, :].bitcast(I32), 1, None,
                                        ALU.logical_shift_right).then_inc(norm_step, 1)
                dve.wait_ge(norm_step, done + GROUP + 3)
                if has_before:
                    dve.wait_ge(feat_ready, (g - 1) * GROUP)
                nc.vector.tensor_scalar(rstd[:, b, :].bitcast(I32), seed[:, :], -1.0, RSQRT_SEED,
                                        ALU.mult, ALU.add).then_inc(norm_step, 1)
                n = done + GROUP + 4
                for _ in range(NEWTON_STEPS):
                    dve.wait_ge(norm_step, n)
                    nc.vector.tensor_tensor(newton[:, :], rstd[:, b, :], rstd[:, b, :], ALU.mult) \
                        .then_inc(norm_step, 1)
                    dve.wait_ge(norm_step, n + 1)
                    nc.vector.scalar_tensor_tensor(out=newton[:, :], in0=newton[:, :], scalar=-0.5,
                                                   in1=var_eps[:, :], op0=ALU.mult, op1=ALU.mult) \
                        .then_inc(norm_step, 1)
                    dve.wait_ge(norm_step, n + 2)
                    nc.vector.scalar_tensor_tensor(out=rstd[:, b, :], in0=newton[:, :], scalar=1.5,
                                                   in1=rstd[:, b, :], op0=ALU.add, op1=ALU.mult) \
                        .then_inc(norm_step, 1)
                    n += 3
                dve.wait_ge(norm_step, n)
                nc.vector.scalar_tensor_tensor(out=shift[:, b, :], in0=mean_var[:, :, 0], scalar=-1.0,
                                               in1=rstd[:, b, :], op0=ALU.mult, op1=ALU.mult) \
                    .then_inc(norm_ready, 1)

            def values(g, b, start):
                done = g * VALUE_STEPS
                dve.wait_ge(d_ready, g + 1)
                if not start:
                    dve.wait_ge(hi_cut, g)
                    dve.wait_ge(lo_cut, g)
                nc.vector.scalar_tensor_tensor(
                    out=scaled_h, in0=h_buf[:, b, :, 0:O], scalar=VALUE_SCALE,
                    in1=d_col[:, b, :].unsqueeze(2).to_broadcast([PART, GROUP, O]),
                    op0=ALU.mult, op1=ALU.mult).then_inc(scaled_ready, 1)
                nc.vector.tensor_copy(s_all[:, :, bass.ts(g, GROUP)],
                                      h_buf[:, b, :, O:O + 2].rearrange("p t s -> p s t")) \
                    .then_inc(value_step, 1)
                nc.vector.tensor_scalar(d_scaled[:, :], d_col[:, b, :], VALUE_SCALE, None, ALU.mult) \
                    .then_inc(value_step, 1)
                dve.wait_ge(value_step, done + 2)
                nc.vector.tensor_copy(value_hi[:, bass.ts(g, GROUP), O], d_scaled[:, :]) \
                    .then_inc(value_step, 1)
                dve.wait_ge(value_step, done + 3)
                nc.vector.tensor_tensor(value_hi[:, bass.ts(g, GROUP), O + 1], d_scaled[:, :],
                                        value_hi[:, bass.ts(g, GROUP), O], ALU.subtract) \
                    .then_inc(value_step, 1)

            def cut_lo(g):
                dve.wait_ge(hi_cut, g + 1)
                nc.vector.tensor_tensor(value_lo[:, bass.ts(g, GROUP), :], scaled_h,
                                        value_hi[:, bass.ts(g, GROUP), 0:O], ALU.subtract) \
                    .then_inc(lo_cut, 1)

            def two_groups(k, first, last):
                for b in range(2):
                    g = 2 * k + b
                    start = first and b == 0
                    for i in range(GROUP):
                        n = g * GROUP + i
                        dve.wait_ge(featT_done, n + 1)
                        if not (start and i < 2):
                            dve.wait_ge(h_done, n - 1)
                        nc.vector.tensor_copy(featT[:, i % 2, :, :].rearrange("p k c -> p (k c)"),
                                              ps_feat[i % 2]).then_inc(featT_ready, 1)
                        if i == 1 and not (last and b == 1):
                            normalise(g + 1, 1 - b, k + b, not start)
                        if i == 4 and not start:
                            values(g - 1, 1 - b, first)
                        if i == 7 and not start:
                            cut_lo(g - 1)

            normalise(0, 0, 0, False)
            in_pairs(dve, GROUPS // 2, two_groups)
            values(GROUPS - 1, 1, False)
            cut_lo(GROUPS - 1)

            dve.wait_ge(value_step, GROUPS * VALUE_STEPS)
            nc.vector.tensor_reduce(ext[:, 0:1], s_all[:, 1, :], op=ALU.max, axis=AX.X).then_inc(ext_step, 1)
            nc.vector.tensor_reduce(ext[:, 1:2], s_all[:, 1, :], op=ALU.min, axis=AX.X).then_inc(ext_step, 1)
            nc.vector.tensor_reduce(ext[:, 2:3], s_all[:, 0, :], op=ALU.min, axis=AX.X).then_inc(ext_step, 1)
            dve.wait_ge(ext_step, 3)
            nc.vector.tensor_scalar(ext[:, 1:3], ext[:, 1:3], -1.0, None, ALU.mult).then_inc(ext_ready, 1)
            dve.wait_ge(extT_done, 1)
            nc.vector.tensor_reduce(row_max[:, :], ps_small[0:3, 0:PART], op=ALU.max, axis=AX.X) \
                .then_inc(ext_step, 1)
            dve.wait_ge(ext_step, 4)
            nc.vector.tensor_scalar(row_diag[:, :], ident[0:3, 0:3], row_max[:, 0:1], None, ALU.mult) \
                .then_inc(diag_ready, 1)
            dve.wait_ge(glob_done, 1)
            nc.vector.tensor_scalar(u_bias[:, :], ps_small[:, PART:PART + 1], SLOPE - 1.0,
                                    math.log(WEIGHT_SCALE), ALU.mult, ALU.add).then_inc(bias_ready, 1)

            def pick_r(t, b):
                nc.vector.tensor_copy(r_cur[:, b:b + 1], r_all[:, bass.ds(t, 1)]).then_inc(r_picked, 1)

            def weigh(t, b, c):
                if c == 0:
                    pick_r(t, b)
                    dve.wait_ge(r_picked, t + 1)
                dve.wait_ge(mask_ready, CHUNKS * t + c + 1)
                nc.vector.scalar_tensor_tensor(out=p_buf[:, c % 2, 0:CHUNK],
                                               in0=u_bc[:, c * CHUNK:(c + 1) * CHUNK],
                                               scalar=r_cur[:, b:b + 1], in1=mask[:, c % 2, :],
                                               op0=ALU.max, op1=ALU.mult).then_inc(p_ready, 1)

            def cut_p(t, c):
                s = STAGES * t + c
                dve.wait_ge(hi_ready, s + 1)
                nc.vector.scalar_tensor_tensor(out=pT_lo[:, c % SPLITS, :], in0=ps_t[c % PSLOTS][:, :],
                                               scalar=0.0, in1=pT_hi[:, c % SPLITS, :],
                                               op0=ALU.max, op1=ALU.subtract).then_inc(lo_ready, 1)

            EPI = 5

            def finish_y(t, b, k):
                done = t * EPI
                dve.wait_ge(stage_summed, STAGES * t + STAGES)
                nc.vector.tensor_reduce(den[:, 0:1], acc[b][:, O:O + 2], op=ALU.add, axis=AX.X) \
                    .then_inc(epi_step, 1)
                dve.wait_ge(epi_step, done + 1)
                nc.vector.tensor_scalar(den[:, 1:2], den[:, 0:1], 0.0, None, ALU.is_equal) \
                    .then_inc(epi_step, 1)
                dve.wait_ge(epi_step, done + 2)
                nc.vector.tensor_tensor(den[:, 2:3], den[:, 0:1], den[:, 1:2], ALU.add) \
                    .then_inc(epi_step, 1)
                nc.vector.tensor_scalar(mean_part[:, :], h_mean[:, :], den[:, 1:2], None, ALU.mult) \
                    .then_inc(epi_step, 1)
                dve.wait_ge(epi_step, done + 4)
                nc.vector.reciprocal(den[:, 3:4], den[:, 2:3]).then_inc(epi_step, 1)
                dve.wait_ge(epi_step, done + 5)
                nc.vector.scalar_tensor_tensor(out=y[:, :], in0=acc[b][:, 0:O], scalar=den[:, 3:4],
                                               in1=mean_part[:, :], op0=ALU.mult, op1=ALU.add) \
                    .then_inc(y_ready, 1)
                dve.wait_ge(y_ready, t + 1)
                dve.wait_ge(x_back[b], 16 * k + 16)
                nc.vector.scalar_tensor_tensor(out=x_plus[:, :], in0=y[:, :], scalar=0.0,
                                               in1=x_tile[:, b, :], op0=ALU.max, op1=ALU.add) \
                    .then_inc(xp_ready, 1)

            def finish_out(t, b, k):
                dve.wait_ge(expm_ready, t + 1)
                dve.wait_ge(xp_ready, t + 1)
                dve.wait_ge(out_stored[b], 16 * k + 16)
                nc.vector.scalar_tensor_tensor(out=o_tile[:, b, :], in0=expm[:, :], scalar=-1.0,
                                               in1=x_plus[:, :], op0=ALU.add, op1=ALU.add) \
                    .then_inc(out_ready, 1)

            def pair(k, first, last):
                for b in range(2):
                    t = 2 * k + b
                    for c in range(CHUNKS):
                        cut_p(t, 2 * c)
                        cut_p(t, 2 * c + 1)
                        if c == 1 and not (first and b == 0):
                            finish_y(t - 1, 1 - b, k - 1 + b)
                        if c < 2:
                            weigh(t, b, c + 2)
                        elif not (last and b == 1):
                            weigh(t + 1, 1 - b, c - 2)
                        if c == 3 and not (first and b == 0):
                            finish_out(t - 1, 1 - b, k - 1 + b)

            dve.wait_ge(r_ready, 1)
            for c in range(2):
                dve.wait_ge(u_loaded[c], 16)
                weigh(0, 0, c)
            for c in range(2, CHUNKS):
                dve.wait_ge(u_loaded[c], 16)
            dve.wait_ge(mean_ready, 1)
            in_pairs(dve, PAIRS, pair)
            finish_y(TILES - 1, 1, PAIRS - 1)
            finish_out(TILES - 1, 1, PAIRS - 1)

        @block.tensor
        def _(pe):
            def transpose_feat(g, i, start):
                n = g * GROUP + i
                pe.wait_ge(feat_ready, n + 1)
                if not (start and i < 2):
                    pe.wait_ge(featT_ready, n - 1)
                for k in range(KC):
                    last = nc.tensor.transpose(ps_feat[i % 2][:, k * PART:(k + 1) * PART],
                                               feat[:, i % 4, k * PART:(k + 1) * PART], ident[:, :])
                last.then_inc(featT_done, 1)

            def h_product(g, i, start):
                n = g * GROUP + i
                pe.wait_ge(featT_ready, n + 1)
                if not (start and i < 2):
                    pe.wait_ge(h_ready, n - 1)
                for k in range(KC):
                    last = nc.tensor.matmul(ps_h[i % 2], featT[:, i % 2, k, :], w_ext[:, k, :],
                                            start=(k == 0), stop=(k == KC - 1))
                last.then_inc(h_done, 1)

            def two_groups(k, first, last):
                for b in range(2):
                    g = 2 * k + b
                    start = first and b == 0
                    for i in range(GROUP):
                        transpose_feat(g, i, start)
                        if i > 0:
                            h_product(g, i - 1, start)
                        elif not start:
                            h_product(g - 1, GROUP - 1, False)
                    if last and b == 1:
                        h_product(g, GROUP - 1, False)

            pe.wait_ge(const_ready, 3)
            pe.wait_ge(wa_step, 2 * KC)
            in_pairs(pe, GROUPS // 2, two_groups)

            pe.wait_ge(ext_ready, 1)
            nc.tensor.transpose(ps_small[0:3, 0:PART], ext[:, :], ident[:, :]).then_inc(extT_done, 1)
            pe.wait_ge(diag_ready, 1)
            nc.tensor.matmul(ps_small[:, PART:PART + 3], ones[0:3, :], row_diag[:, :],
                             start=True, stop=True).then_inc(glob_done, 1)
            pe.wait_ge(bias_ready, 1)
            nc.tensor.transpose(ps_small[0:TILES, 256:256 + PART], s_all[:, 1, :], ident[:, :]) \
                .then_inc(s2T_done, 1)
            pe.wait_ge(h_summed, GROUPS + 1)
            for i in range(GROUP):
                last = nc.tensor.matmul(ps_small[:, 512:512 + O], ones[:, :], h_sum[:, i, :],
                                        start=(i == 0), stop=(i == GROUP - 1))
            last.then_inc(mean_done, 1)

            def transpose_p(t, c, start):
                s = STAGES * t + c
                if c % 2 == 0:
                    pe.wait_ge(p_ready, CHUNKS * t + c // 2 + 1)
                if c >= PSLOTS:
                    pe.wait_ge(lo_ready, s - PSLOTS + 1)
                elif not start:
                    before = max(e for e in range(STAGES) if e % PSLOTS == c)
                    pe.wait_ge(lo_ready, s - c - STAGES + before + 1)
                for j in range(BLOCKS):
                    at = (c % 2) * STAGE + j * PART
                    last = nc.tensor.transpose(ps_t[c % PSLOTS][:, j * PART:(j + 1) * PART],
                                               p_buf[:, (c // 2) % 2, at:at + PART], ident[:, :])
                last.then_inc(pT_done, 1)

            def sum_hi(t, b, c, start):
                pe.wait_ge(hi_ready, STAGES * t + c + 1)
                if c == 0 and not start:
                    pe.wait_ge(y_ready, t - 1)
                for j in range(BLOCKS):
                    node = c * BLOCKS + j
                    pT = pT_hi[:, c % SPLITS, j * PART:(j + 1) * PART]
                    nc.tensor.matmul(acc[b][:, 0:O + 2], pT, value_hi[:, node, :],
                                     start=(node == 0), stop=False)
                    nc.tensor.matmul(acc[b][:, 0:O], pT, value_lo[:, node, :], start=False, stop=False)

            def sum_lo(t, b, c):
                pe.wait_ge(lo_ready, STAGES * t + c + 1)
                for j in range(BLOCKS):
                    node = c * BLOCKS + j
                    last = nc.tensor.matmul(acc[b][:, 0:O + 1], pT_lo[:, c % SPLITS, j * PART:(j + 1) * PART],
                                            value_hi[:, node, 0:O + 1], start=False, stop=(node == TILES - 1))
                last.then_inc(stage_summed, 1)

            def pair(k, first, last):
                for b in range(2):
                    t = 2 * k + b
                    for c in range(STAGES):
                        sum_hi(t, b, c, first)
                        if c + 2 < STAGES:
                            transpose_p(t, c + 2, first and b == 0)
                        elif not (last and b == 1):
                            transpose_p(t + 1, c + 2 - STAGES, False)
                        sum_lo(t, b, c)

            pe.wait_ge(mean_ready, 1)
            pe.wait_ge(h_ready, TILES)
            pe.wait_ge(lo_cut, GROUPS)
            pe.wait_ge(value_step, GROUPS * VALUE_STEPS)
            transpose_p(0, 0, True)
            transpose_p(0, 1, True)
            in_pairs(pe, PAIRS, pair)


_INS = ['x', 'adj', 'L0_gnn_W', 'L0_gnn_attn']


def kernel(**inputs):
    import numpy as _np
    import concourse.bacc as _bacc
    from concourse import mybir as _mybir
    from concourse.bass_utils import run_bass_kernel_spmd as _run

    nc = _bacc.Bacc("TRN2", target_bir_lowering=False, num_devices=1)
    arrays, args = {}, []
    for name in _INS:
        a = _np.ascontiguousarray(inputs[name])
        arrays[f"in_{name}_dram"] = a
        args.append(nc.dram_tensor(f"in_{name}_dram", a.shape, _mybir.dt.from_np(a.dtype), kind="ExternalInput").ap())
    x = arrays["in_x_dram"]
    args.append(nc.dram_tensor("out_dram", x.shape, _mybir.dt.from_np(x.dtype), kind="ExternalOutput").ap())
    gat_kernel(nc, *args)
    r = _run(nc, [arrays], core_ids=[0])
    return r.results[0]["out_dram"]
```

```python
import concourse.bass as bass
from concourse import mybir
from contextlib import ExitStack
import math

FP32 = mybir.dt.float32
FP16 = mybir.dt.float16
FP8 = mybir.dt.float8e4
BF16 = mybir.dt.bfloat16
I32 = mybir.dt.int32
ALU = mybir.AluOpType
ACT = mybir.ActivationFunctionType
AX = mybir.AxisListType

PART = 128
SLOPE = 0.2
LN_EPS = 1e-5
VALUE_SCALE = 256.0
WEIGHT_SCALE = 1024.0
S2_LIMIT = 10.0
S1_LIMIT = 5.0
SPREAD_LIMIT = 9.0
NORM_LIMIT = 4.5
NORM_LEAST = 1.0 / 256
MASKED = 9e15
RSQRT_SEED = float(0x5F3759DF)
NEWTON_STEPS = 3


def gat_kernel(nc, x, adj, W, attn, out):
    N, F = x.shape
    O = W.shape[1]
    TILES = N // PART
    GROUP = 8
    GROUPS = TILES // GROUP
    KC = F // PART
    HC = O + 2
    RING = 4
    ROWS = 4
    QUADS = TILES // ROWS
    WIDE = ROWS * PART
    PIECE = 512
    PIECES = N // PIECE
    BLOCKS = 2
    STAGES = TILES // BLOCKS
    PER_PIECE = PIECE // (BLOCKS * PART)
    VALUE_STEPS = 4
    AHEAD = 4

    x_tiles = x.rearrange("(m p k) f -> p m (k f)", p=PART, k=ROWS)
    adj_tiles = adj.rearrange("(m p k) n -> p m k n", p=PART, k=ROWS)
    out_tiles = out.rearrange("(m p k) f -> p m (k f)", p=PART, k=ROWS)
    attn_rows = attn.rearrange("(two n) one -> one two n", two=2)

    CHUNK = 2048
    CHUNKS = N // CHUNK
    FOUR = TILES // 4

    h_dram = nc.dram_tensor("h_all", [PART, TILES, O], FP32).ap()
    s2_dram = nc.dram_tensor("s2_row", [TILES, PART], FP32).ap()
    r_dram = nc.dram_tensor("r_row", [TILES, PART], FP32).ap()

    ctx = ExitStack()
    with ctx:
        def sb(name, shape, dt):
            return ctx.enter_context(nc.sbuf_tensor(name, shape, dt))

        def sem(name):
            return ctx.enter_context(nc.semaphore(name))

        ident = sb("ident", [PART, PART], FP32)
        ident_bf = sb("ident_bf", [PART, PART], BF16)
        ones = sb("ones", [PART, PART], FP32)
        minus_half = sb("minus_half", [PART, 1], FP32)
        w_ext = sb("w_ext", [PART, KC, HC], FP32)
        s_all = sb("s_all", [PART, 2, TILES], FP32)
        u_col = sb("u_col", [PART, TILES], FP32)
        h_mean = sb("h_mean", [PART, O], FP32)
        EXT = 5
        ext = sb("ext", [PART, EXT], FP32)
        row_max = sb("row_max", [EXT, 1], FP32)
        row_diag = sb("row_diag", [EXT, EXT], FP32)
        glob = sb("glob", [PART, EXT], FP32)
        over = sb("over", [PART, 6], FP32)
        over_any = sb("over_any", [PART, 1], I32)
        w_sq = sb("w_sq", [PART, KC, O], FP32)
        ur_bias = sb("ur_bias", [PART, 1], FP32)
        rT = sb("rT", [TILES, PART], FP32)
        values = sb("values", [PART, TILES * (2 * O + 2)], FP16)
        value_lo = values[:, 0:TILES * O].rearrange("p (t f) -> p t f", t=TILES)
        value_hi = values[:, TILES * O:].rearrange("p (t f) -> p t f", t=TILES)

        arena = sb("arena", [PART, TILES * F], FP32)
        x_in = arena[:, :].rearrange("p (t f) -> p t f", t=TILES)
        ADJ = RING * ROWS * PIECE
        MASK = ADJ // 4
        CUT = RING * BLOCKS * WIDE // 2
        adj_in = arena[:, 0:ADJ].bitcast(I32).rearrange("p (b r c) -> p b r c", b=RING, r=ROWS)
        mask = arena[:, ADJ:ADJ + MASK].bitcast(FP8).rearrange("p (b r c) -> p b r c", b=RING, r=ROWS)
        mask_pairs = arena[:, ADJ:ADJ + MASK].bitcast(BF16).rearrange(
            "p (b r c two) -> p b r two c", b=RING, r=ROWS, two=PER_PIECE)
        pT_hi = arena[:, ADJ + MASK:ADJ + MASK + CUT].bitcast(FP16).rearrange("p (b w) -> p b w", b=RING)
        pT_lo = arena[:, ADJ + MASK + CUT:ADJ + MASK + 2 * CUT].bitcast(FP16) \
            .rearrange("p (b w) -> p b w", b=RING)

        arena2 = sb("arena2", [PART, 2 * GROUP * (HC + O)], FP32)
        H = 2 * GROUP * HC
        h_buf = arena2[:, 0:H].rearrange("p (b t f) -> p b t f", b=2, t=GROUP)
        scaled_h = arena2[:, H:H + GROUP * O].rearrange("p (t f) -> p t f", t=GROUP)
        h_sum = arena2[:, H + GROUP * O:H + 2 * GROUP * O].rearrange("p (t f) -> p t f", t=GROUP)
        HALF = 2 * BLOCKS * WIDE
        Q = ROWS * O
        at = HALF
        acc_sb = arena2[:, at:at + ROWS * (O + 2)].rearrange("p (r f) -> p r f", r=ROWS)
        at += ROWS * (O + 2)
        y = arena2[:, at:at + Q]
        expm = arena2[:, at + Q:at + 2 * Q]
        x_plus = arena2[:, at + 2 * Q:at + 3 * Q]
        weighted = arena[:, ADJ + MASK + 2 * CUT:ADJ + MASK + 2 * CUT + Q]
        elu_neg = arena[:, ADJ + MASK + 2 * CUT + Q:ADJ + MASK + 2 * CUT + 2 * Q]

        arena3 = sb("arena3", [PART, 2 * RING * F], FP32)
        feat = arena3[:, 0:RING * F].rearrange("p (b f) -> p b f", b=RING)
        featT = arena3[:, RING * F:2 * RING * F].rearrange("p (b f) -> p b f", b=RING)
        pT = [half[:, i * BLOCKS * WIDE:(i + 1) * BLOCKS * WIDE] for half in (arena2, arena3) for i in range(2)]

        r_in = sb("r_in", [PART, WIDE], FP32)
        r_bc = sb("r_bc", [PART, WIDE], FP32)
        x_quad = sb("x_quad", [PART, Q], FP32)
        pos_part = sb("pos_part", [PART, Q], FP32)
        neg_part = sb("neg_part", [PART, Q], FP32)
        out_quad = sb("out_quad", [PART, Q], FP32)
        mean_part = sb("mean_part", [PART, Q], FP32)
        den = sb("den", [PART, 4, ROWS], FP32)

        h_all = values[:, 0:TILES * 2 * O].bitcast(FP32).rearrange("p (t f) -> p t f", t=TILES)
        s2_bc = arena[:, 0:N]
        score = arena[:, N:2 * N]
        g_adj = arena2[:, 0:CHUNK].bitcast(I32)
        edge = arena2[:, CHUNK:2 * CHUNK]
        raw = arena2[:, 2 * CHUNK:3 * CHUNK]
        leaky = arena2[:, 3 * CHUNK:4 * CHUNK]
        wT = arena3[:, 0:2 * 4 * PART].rearrange("p (b w) -> p b w", b=2)
        s2T = sb("s2T", [TILES, PART], FP32)
        s1_cur = sb("s1_cur", [PART, 1], FP32)
        neg_max = sb("neg_max", [PART, 2], FP32)
        g_den = sb("g_den", [PART, 2], FP32)

        attn_bc = sb("attn_bc", [PART, 2, O], FP32)
        scratch = sb("scratch", [PART, O], FP32)
        stats = sb("stats", [PART, GROUP, 6], FP32)
        mean_var = sb("mean_var", [PART, GROUP, 2], FP32)
        var_eps = sb("var_eps", [PART, GROUP], FP32)
        seed = sb("seed", [PART, GROUP], I32)
        newton = sb("newton", [PART, GROUP], FP32)
        rstd = sb("rstd", [PART, 2, GROUP], FP32)
        shift = sb("shift", [PART, 2, GROUP], FP32)
        d_col = sb("d_col", [PART, 2, GROUP], FP32)
        d_scaled = sb("d_scaled", [PART, 2, GROUP], FP32)

        ring = [ctx.enter_context(nc.psum_tensor(f"ring{i}", [PART, 512], FP32)) for i in range(RING)]
        acc = [ctx.enter_context(nc.psum_tensor(f"acc{i}", [PART, 512], FP32)) for i in range(ROWS)]
        ps_pairs = [ring[i][:, :].bitcast(BF16)[:, 0:WIDE] for i in range(RING)]
        ps_mask = [ring[i][:, 0:WIDE // 2].bitcast(FP8).rearrange("p (w two) -> p two w", two=BLOCKS)
                   for i in range(RING)]
        ps_feat = [ring[i][:, 0:F] for i in range(RING)]
        ps_h = [acc[i][:, 0:HC] for i in range(RING)]
        ps_norm = ring[RING - 1][:, F:F + O]
        ps_ext = ring[0]
        ps_s = ring[1]
        ps_mean = ring[2]

        w_loaded = sem("w_loaded")
        const_ready = sem("const_ready")
        wa_step = sem("wa_step")
        x_loaded = [sem("x_loaded0"), sem("x_loaded1")]
        norm_step = sem("norm_step")
        norm_ready = sem("norm_ready")
        feat_ready = sem("feat_ready")
        featT_done = sem("featT_done")
        featT_ready = sem("featT_ready")
        h_done = sem("h_done")
        h_ready = sem("h_ready")
        d_ready = sem("d_ready")
        value_step = sem("value_step")
        scaled_ready = sem("scaled_ready")
        hi_cut = sem("hi_cut")
        lo_cut = sem("lo_cut")
        h_summed = sem("h_summed")
        ext_ready = sem("ext_ready")
        ext_step = sem("ext_step")
        extT_done = sem("extT_done")
        sT_done = sem("sT_done")
        diag_ready = sem("diag_ready")
        glob_done = sem("glob_done")
        bias_ready = sem("bias_ready")
        rT_ready = sem("rT_ready")
        u_ready = sem("u_ready")
        r_stored = sem("r_stored")
        mean_done = sem("mean_done")
        mean_ready = sem("mean_ready")

        h_stored = [sem("h_stored0"), sem("h_stored1")]
        norms_done = sem("norms_done")
        norms_read = sem("norms_read")
        glob_read = sem("glob_read")
        over_step = sem("over_step")
        over_ready = sem("over_ready")

        g_h_loaded = sem("g_h_loaded")
        g_s2T_done = sem("g_s2T_done")
        g_s2T_ready = sem("g_s2T_ready")
        g_s2_stored = sem("g_s2_stored")
        g_s2_loaded = sem("g_s2_loaded")
        g_x_loaded = sem("g_x_loaded")
        g_adj_loaded = sem("g_adj_loaded")
        g_adj_read = sem("g_adj_read")
        g_step = sem("g_step")
        g_top_ready = sem("g_top_ready")
        g_max_ready = sem("g_max_ready")
        g_w_ready = sem("g_w_ready")
        g_wT_done = sem("g_wT_done")
        g_wT_ready = sem("g_wT_ready")
        g_summed = sem("g_summed")
        g_rden_ready = sem("g_rden_ready")
        g_y_ready = sem("g_y_ready")
        g_neg_ready = sem("g_neg_ready")
        g_expm_ready = sem("g_expm_ready")
        g_xp_ready = sem("g_xp_ready")
        g_out_ready = sem("g_out_ready")
        g_out_stored = sem("g_out_stored")

        adj_loaded = [sem(f"adj_loaded{i}") for i in range(RING)]
        r_loaded = sem("r_loaded")
        r_ready = sem("r_ready")
        mask_ready = sem("mask_ready")
        pT_done = sem("pT_done")
        p_ready = sem("p_ready")
        hi_ready = sem("hi_ready")
        lo_ready = sem("lo_ready")
        stage_summed = sem("stage_summed")
        row_summed = sem("row_summed")
        acc_copied = [sem(f"acc_copied{r}") for r in range(ROWS)]
        epi_step = sem("epi_step")
        flag_ready = sem("flag_ready")
        rden_ready = sem("rden_ready")
        weighted_ready = sem("weighted_ready")
        pos_ready = sem("pos_ready")
        elu_ready = sem("elu_ready")
        y_ready = sem("y_ready")
        neg_ready = sem("neg_ready")
        expm_ready = sem("expm_ready")
        xp_ready = sem("xp_ready")
        out_ready = sem("out_ready")
        x_back = sem("x_back")
        out_stored = sem("out_stored")

        block = ctx.enter_context(nc.Block())

        def rounds(eng, count, one):
            one(0, True, False)
            with eng.Fori(1, count - 1) as k:
                one(k, False, False)
            one(count - 1, False, True)

        def in_general(eng, general):
            eng.wait_ge(over_ready, 1)
            with eng.If(eng.value_load(over_any[0:1, 0:1], min_val=0, max_val=1) != 0):
                general()

        @block.sync
        def _(sync):
            def load_x(k, first, last):
                for b in range(2):
                    if not first:
                        sync.wait_ge(x_loaded[b], 16 * k)
                    sync.dma_start(x_in[:, bass.ts(2 * k + b, GROUP), :]
                                   .rearrange("p (m k) f -> p m (k f)", k=ROWS),
                                   x_tiles[:, bass.ts(2 * k + b, GROUP // ROWS), :]).then_inc(x_loaded[b], 16)

            def load_adj(q, e):
                sync.dma_start(adj_in[:, e % RING, :, :],
                               adj_tiles[:, bass.ds(q, 1), :, e * PIECE:(e + 1) * PIECE]
                               .rearrange("p m k c -> p (m k) c")) \
                    .then_inc(adj_loaded[e % RING], 16)

            load_x(0, True, False)

            def store_h(k):
                for b in range(2):
                    g = 2 * k + b
                    sync.wait_ge(h_ready, (g + 1) * GROUP)
                    sync.dma_start(h_dram[:, bass.ts(g, GROUP), :], h_buf[:, b, :, 0:O]) \
                        .then_inc(h_stored[b], 16)

            with sync.Fori(1, GROUPS // 2) as k:
                load_x(k, False, False)
                store_h(k - 1)

            sync.wait_ge(feat_ready, TILES // 2)
            for e in range(RING):
                load_adj(0, e)
            store_h(GROUPS // 2 - 1)

            sync.wait_ge(rT_ready, 1)
            sync.dma_start(r_dram, rT[:, :]).then_inc(r_stored, 16)
            sync.wait_ge(r_stored, 16)
            r_rows = r_dram.rearrange("(q r) p -> q (r p)", r=ROWS)

            def quad(q, first, last):
                if first:
                    sync.dma_start(r_in[:, :], r_rows[0:1, :].to_broadcast([PART, WIDE])).then_inc(r_loaded, 16)
                if not last:
                    sync.wait_ge(r_ready, q + 1)
                    sync.dma_start(r_in[:, :], r_rows[bass.ds(q + 1, 1), :].to_broadcast([PART, WIDE])) \
                        .then_inc(r_loaded, 16)
                for e in range(PIECES):
                    if e + RING < PIECES:
                        sync.wait_ge(mask_ready, PIECES * q + e + 1)
                        load_adj(q, e + RING)
                    elif not last:
                        sync.wait_ge(mask_ready, PIECES * q + e + 1)
                        load_adj(q + 1, e + RING - PIECES)
                    if e == 7:
                        if not first:
                            sync.wait_ge(out_ready, q)
                            sync.dma_start(out_tiles[:, bass.ds(q - 1, 1), :],
                                           out_quad[:, :].rearrange("p (m f) -> p m f", m=1)) \
                                .then_inc(out_stored, 16)
                            sync.wait_ge(xp_ready, q)
                        sync.dma_start(x_quad[:, :].rearrange("p (m f) -> p m f", m=1),
                                       x_tiles[:, bass.ds(q, 1), :]).then_inc(x_back, 16)

            rounds(sync, QUADS, quad)
            sync.wait_ge(out_ready, QUADS)
            sync.dma_start(out_tiles[:, QUADS - 1, :], out_quad[:, :]).then_inc(out_stored, 16)
            sync.wait_ge(out_stored, 16 * QUADS + 16)

            x_rows, adj_rows, out_rows = (a.rearrange("(m p k) n -> m k p n", p=PART, k=ROWS)
                                          for a in (x, adj, out))

            def tile_in_general(m, k):
                t = ROWS * m + k
                sync.dma_start(x_quad[:, 0:F], x_rows[bass.ds(m, 1), k, :, :].rearrange("m p f -> (m p) f")) \
                    .then_inc(g_x_loaded, 16)
                for c in range(CHUNKS):
                    if c > 0:
                        sync.wait_ge(g_adj_read, CHUNKS * t + c)
                    sync.dma_start(g_adj, adj_rows[bass.ds(m, 1), k, :, c * CHUNK:(c + 1) * CHUNK]
                                   .rearrange("m p n -> (m p) n")).then_inc(g_adj_loaded, 16)
                sync.wait_ge(g_out_ready, t + 1)
                sync.dma_start(out_rows[bass.ds(m, 1), k, :, :].rearrange("m p f -> (m p) f"),
                               out_quad[:, 0:O]).then_inc(g_out_stored, 16)
                sync.wait_ge(g_out_stored, 16 * t + 16)
                sync.nop(nofuse=True)

            def general():
                for b in range(2):
                    sync.wait_ge(h_stored[b], 16 * (GROUPS // 2))
                sync.dma_start(h_all, h_dram).then_inc(g_h_loaded, 16)
                sync.wait_ge(g_s2T_ready, 1)
                sync.dma_start(s2_dram, s2T[:, :]).then_inc(g_s2_stored, 16)
                sync.wait_ge(g_s2_stored, 16)
                s2_row = s2_dram.rearrange("(one t) p -> one (t p)", one=1)
                sync.dma_start(s2_bc, s2_row.to_broadcast([PART, N])).then_inc(g_s2_loaded, 16)
                with sync.Fori(0, QUADS) as m:
                    for k in range(ROWS):
                        tile_in_general(m, k)

            in_general(sync, general)

        @block.gpsimd
        def _(pool):
            pool.memset(ones[:, :], 1.0).then_inc(const_ready, 1)
            pool.memset(ident[:, :], 0.0).then_inc(const_ready, 1)
            pool.wait_ge(const_ready, 2)
            pool.affine_select(out=ident[:, :], in_=ident[:, :], compare_op=ALU.not_equal, fill=1.0,
                               base=0, pattern=[[-1, PART]], channel_multiplier=1).then_inc(const_ready, 1)
            pool.wait_ge(const_ready, 3)
            pool.tensor_copy(ident_bf[:, :], ident[:, :]).then_inc(const_ready, 1)
            pool.memset(minus_half[:, :], -0.5).then_inc(const_ready, 1)
            pool.memset(out_quad[:, :], 0.0).then_inc(out_stored, 16)
            pool.memset(h_sum, 0.0).then_inc(h_summed, 1)

            def two_groups(k, first, last):
                for b in range(2):
                    g = 2 * k + b
                    pool.wait_ge(value_step, g * VALUE_STEPS + 1)
                    if not (first and b == 0):
                        pool.wait_ge(lo_cut, g)
                    nc.gpsimd.tensor_tensor(scaled_h, h_buf[:, b, :, 0:O],
                                            d_scaled[:, b, :].unsqueeze(2).to_broadcast([PART, GROUP, O]),
                                            ALU.mult).then_inc(scaled_ready, 1)
                    pool.wait_ge(h_summed, g + 1)
                    nc.gpsimd.tensor_tensor(h_sum, h_sum, h_buf[:, b, :, 0:O], ALU.add) \
                        .then_inc(h_summed, 1)

            rounds(pool, GROUPS // 2, two_groups)

            with pool.Fori(0, QUADS) as q:
                pool.wait_ge(weighted_ready, q + 1)
                nc.gpsimd.tensor_tensor(y, weighted, mean_part[:, :], ALU.add).then_inc(y_ready, 1)
                pool.wait_ge(pos_ready, q + 1)
                pool.wait_ge(x_back, 16 * q + 16)
                nc.gpsimd.tensor_tensor(x_plus, pos_part[:, :], x_quad[:, :], ALU.add).then_inc(xp_ready, 1)
                pool.wait_ge(expm_ready, q + 1)
                pool.nop(nofuse=True)
                nc.gpsimd.tensor_scalar(elu_neg, expm, -1.0, 1.0, ALU.add, ALU.mult).then_inc(elu_ready, 1)
                pool.wait_ge(elu_ready, q + 1)
                pool.wait_ge(xp_ready, q + 1)
                pool.wait_ge(out_stored, 16 * q + 16)
                nc.gpsimd.tensor_tensor(out_quad[:, :], elu_neg, x_plus, ALU.add).then_inc(out_ready, 1)

        @block.scalar
        def _(act):
            for k in range(KC):
                act.dma_start(w_ext[:, k, 0:O], W[k * PART:(k + 1) * PART, :]).then_inc(w_loaded, 16)
            act.dma_start(attn_bc[:, :, :], attn_rows.to_broadcast([PART, 2, O])).then_inc(w_loaded, 16)

            LAG = 3

            def h_out(g, b, i, first, pair_no):
                act.wait_ge(h_done, g * GROUP + i + 1)
                if i == 0 and not first:
                    act.wait_ge(scaled_ready, g - 1)
                    act.wait_ge(value_step, (g - 1) * VALUE_STEPS)
                    act.wait_ge(h_summed, g)
                    act.wait_ge(h_stored[b], 16 * pair_no)
                nc.scalar.activation(h_buf[:, b, i, :], ps_h[i % RING], ACT.Copy).then_inc(h_ready, 1)

            def make_d(g, b):
                act.wait_ge(h_ready, (g + 1) * GROUP)
                nc.scalar.activation(d_col[:, b, :], h_buf[:, b, :, O + 1], ACT.Exp, scale=SLOPE) \
                    .then_inc(d_ready, 1)

            def cut_hi(g):
                act.wait_ge(scaled_ready, g + 1)
                nc.scalar.activation(value_hi[:, bass.ts(g, GROUP), 0:O], scaled_h, ACT.Copy) \
                    .then_inc(hi_cut, 1)

            def two_groups(k, first, last):
                for b in range(2):
                    g = 2 * k + b
                    start = first and b == 0
                    for i in range(GROUP):
                        if i == 0:
                            act.wait_ge(norm_ready, g + 1)
                        if not (start and i < RING):
                            act.wait_ge(featT_done, g * GROUP + i - RING + 1)
                        nc.scalar.activation(feat[:, i % RING, :], x_in[:, g * GROUP + i, :], ACT.Relu,
                                             bias=shift[:, b, i:i + 1], scale=rstd[:, b, i:i + 1]) \
                            .then_inc(feat_ready, 1)
                        if i >= LAG:
                            h_out(g, b, i - LAG, first, k)
                        elif not start:
                            h_out(g - 1, 1 - b, i - LAG + GROUP, first, k)
                        if i == LAG - 1 and not start:
                            make_d(g - 1, 1 - b)
                        if i == 7 and not start:
                            cut_hi(g - 1)
                    if last and b == 1:
                        for i in range(GROUP - LAG, GROUP):
                            h_out(g, b, i, first, k)
                        make_d(g, b)

            rounds(act, GROUPS // 2, two_groups)

            act.wait_ge(bias_ready, 1)
            act.wait_ge(sT_done, 1)
            nc.scalar.activation(rT[:, :], ps_s[0:TILES, 0:PART], ACT.Exp, bias=ur_bias[0:TILES, 0:1],
                                 scale=SLOPE - 1.0).then_inc(rT_ready, 1)
            nc.scalar.activation(u_col[:, :], s_all[:, 1, :], ACT.Exp, bias=ur_bias[:, 0:1],
                                 scale=1.0 - SLOPE).then_inc(u_ready, 1)

            def make_mask(q, e, start):
                act.wait_ge(adj_loaded[e % RING], 16 * (PIECES // RING) * q + 16 * (e // RING) + 16)
                if not (start and e < RING):
                    act.wait_ge(pT_done, PER_PIECE * (PIECES * q + e - RING + 1))
                act.nop(nofuse=True)
                nc.scalar.activation(mask[:, e % RING, :, :], adj_in[:, e % RING, :, :], ACT.Sign,
                                     bias=minus_half[:, 0:1], saturate=False) \
                    .then_inc(mask_ready, 1)

            act.wait_ge(const_ready, 5)
            for e in range(RING - 1):
                make_mask(0, e, True)
            cut_hi(GROUPS - 1)
            act.wait_ge(mean_done, 1)
            nc.scalar.activation(h_mean[:, :], ps_mean[:, 0:O], ACT.Copy, scale=1.0 / N) \
                .then_inc(mean_ready, 1)

            def copy_acc(q, r):
                if r < ROWS - 1:
                    act.wait_ge(row_summed, (ROWS - 1) * q + r + 1)
                else:
                    act.wait_ge(stage_summed, STAGES * q + STAGES)
                nc.scalar.activation(acc_sb[:, r, :], acc[r][:, 0:O + 2], ACT.Copy) \
                    .then_inc(acc_copied[r], 1)

            def rows_y(q):
                act.wait_ge(rden_ready, q + 1)
                for r in range(ROWS):
                    part = slice(r * O, (r + 1) * O)
                    nc.scalar.activation(weighted[:, part], acc_sb[:, r, 0:O], ACT.Copy,
                                         scale=den[:, 3, r:r + 1])
                    last = nc.scalar.activation(mean_part[:, part], h_mean[:, :], ACT.Copy,
                                                scale=den[:, 1, r:r + 1])
                last.then_inc(weighted_ready, 1)

            def elu_exp(q):
                act.wait_ge(y_ready, q + 1)
                nc.scalar.activation(pos_part[:, :], y, ACT.Relu).then_inc(pos_ready, 1)
                nc.scalar.activation(neg_part[:, :], y, ACT.Relu, scale=-1.0).then_inc(neg_ready, 1)
                act.wait_ge(neg_ready, q + 1)
                nc.scalar.activation(expm, neg_part[:, :], ACT.Exp, scale=-1.0).then_inc(expm_ready, 1)

            def quad(q, first, last):
                for c in range(STAGES):
                    s = STAGES * q + c
                    act.wait_ge(p_ready, s + 1)
                    if not (first and c < RING):
                        act.wait_ge(stage_summed, s - RING + 1)
                    nc.scalar.activation(pT_hi[:, c % RING, :], pT[c % RING], ACT.Relu) \
                        .then_inc(hi_ready, 1)
                    if c == 1 and not first:
                        for r in range(ROWS):
                            copy_acc(q - 1, r)
                    if c == 5 and not first:
                        rows_y(q - 1)
                    if c % PER_PIECE == 0:
                        e = c // PER_PIECE + RING - 1
                        if e < PIECES:
                            make_mask(q, e, first)
                        elif not last:
                            make_mask(q + 1, e - PIECES, False)
                    if c == 11 and not first:
                        elu_exp(q - 1)

            rounds(act, QUADS, quad)
            for r in range(ROWS):
                copy_acc(QUADS - 1, r)
            rows_y(QUADS - 1)
            elu_exp(QUADS - 1)

            def general():
                with act.Fori(0, TILES) as t:
                    act.wait_ge(g_max_ready, t + 1)
                    nc.scalar.activation(score, score, ACT.Exp, bias=neg_max[:, 1:2],
                                         accum_out=g_den[:, 0:1]).then_inc(g_w_ready, 1)
                    act.wait_ge(g_y_ready, t + 1)
                    nc.scalar.activation(neg_part[:, 0:O], mean_part[:, 0:O], ACT.Relu, scale=-1.0) \
                        .then_inc(g_neg_ready, 1)
                    act.wait_ge(g_neg_ready, t + 1)
                    nc.scalar.activation(neg_part[:, O:2 * O], neg_part[:, 0:O], ACT.Exp, scale=-1.0) \
                        .then_inc(g_expm_ready, 1)

            in_general(act, general)

        @block.vector
        def _(dve):
            NORM = GROUP + 4 + 3 * NEWTON_STEPS

            def measure(g, b, k, i):
                if i == 0:
                    dve.wait_ge(x_loaded[b], 16 * k + 16)
                nc.vector.bn_stats(stats[:, i, :], x_in[:, g * GROUP + i, :]).then_inc(norm_step, 1)

            def normalise(g, b, part, has_before):
                done = g * NORM
                if part == 0:
                    dve.wait_ge(norm_step, done + GROUP)
                    dve.nop(nofuse=True)
                    for i in range(GROUP):
                        last = nc.vector.bn_aggr(mean_var[:, i, :], stats[:, i, :])
                    last.then_inc(norm_step, 1)
                    dve.wait_ge(norm_step, done + GROUP + 1)
                    nc.vector.tensor_scalar(var_eps[:, :], mean_var[:, :, 1], LN_EPS, None, ALU.add) \
                        .then_inc(norm_step, 1)
                    dve.wait_ge(norm_step, done + GROUP + 2)
                    nc.vector.tensor_scalar(seed[:, :], var_eps[:, :].bitcast(I32), 1, None,
                                            ALU.logical_shift_right).then_inc(norm_step, 1)
                    dve.wait_ge(norm_step, done + GROUP + 3)
                    if has_before:
                        dve.wait_ge(feat_ready, (g - 1) * GROUP)
                    nc.vector.tensor_scalar(rstd[:, b, :].bitcast(I32), seed[:, :], -1.0, RSQRT_SEED,
                                            ALU.mult, ALU.add).then_inc(norm_step, 1)
                    return
                n = done + GROUP + 4 + 3 * (part - 1)
                dve.wait_ge(norm_step, n)
                nc.vector.tensor_tensor(newton[:, :], rstd[:, b, :], rstd[:, b, :], ALU.mult) \
                    .then_inc(norm_step, 1)
                dve.wait_ge(norm_step, n + 1)
                nc.vector.scalar_tensor_tensor(out=newton[:, :], in0=newton[:, :], scalar=-0.5,
                                               in1=var_eps[:, :], op0=ALU.mult, op1=ALU.mult) \
                    .then_inc(norm_step, 1)
                dve.wait_ge(norm_step, n + 2)
                nc.vector.scalar_tensor_tensor(out=rstd[:, b, :], in0=newton[:, :], scalar=1.5,
                                               in1=rstd[:, b, :], op0=ALU.add, op1=ALU.mult) \
                    .then_inc(norm_step, 1)
                if part == NEWTON_STEPS:
                    dve.wait_ge(norm_step, n + 3)
                    nc.vector.scalar_tensor_tensor(out=shift[:, b, :], in0=mean_var[:, :, 0], scalar=-1.0,
                                                   in1=rstd[:, b, :], op0=ALU.mult, op1=ALU.mult) \
                        .then_inc(norm_ready, 1)

            def keep_scores(g, b):
                done = g * VALUE_STEPS
                dve.wait_ge(d_ready, g + 1)
                nc.vector.tensor_scalar(d_scaled[:, b, :], d_col[:, b, :], VALUE_SCALE, None, ALU.mult) \
                    .then_inc(value_step, 1)
                nc.vector.tensor_copy(s_all[:, :, bass.ts(g, GROUP)],
                                      h_buf[:, b, :, O:O + 2].rearrange("p t s -> p s t")) \
                    .then_inc(value_step, 1)
                dve.wait_ge(value_step, done + 1)
                nc.vector.tensor_copy(value_hi[:, bass.ts(g, GROUP), O], d_scaled[:, b, :]) \
                    .then_inc(value_step, 1)
                dve.wait_ge(value_step, done + 3)
                nc.vector.tensor_tensor(value_hi[:, bass.ts(g, GROUP), O + 1], d_scaled[:, b, :],
                                        value_hi[:, bass.ts(g, GROUP), O], ALU.subtract) \
                    .then_inc(value_step, 1)

            def cut_lo(g):
                dve.wait_ge(hi_cut, g + 1)
                nc.vector.tensor_tensor(value_lo[:, bass.ts(g, GROUP), :], scaled_h,
                                        value_hi[:, bass.ts(g, GROUP), 0:O], ALU.subtract) \
                    .then_inc(lo_cut, 1)

            def two_groups(k, first, last):
                for b in range(2):
                    g = 2 * k + b
                    start = first and b == 0
                    ahead = not (last and b == 1)
                    for i in range(GROUP):
                        n = g * GROUP + i
                        dve.wait_ge(featT_done, n + 1)
                        if not (start and i < RING):
                            dve.wait_ge(h_done, n - RING + 1)
                        if start and i == RING - 1:
                            dve.wait_ge(norms_done, 1)
                            nc.vector.tensor_reduce(ext[:, 3:4], ps_norm, op=ALU.max, axis=AX.X) \
                                .then_inc(norms_read, 1)
                            nc.vector.tensor_reduce(ext[:, 4:5], ps_norm, op=ALU.min, axis=AX.X) \
                                .then_inc(norms_read, 1)
                        nc.vector.tensor_copy(featT[:, i % RING, :], ps_feat[i % RING]) \
                            .then_inc(featT_ready, 1)
                        if i < 4 and ahead:
                            measure(g + 1, 1 - b, k + b, 2 * i)
                            measure(g + 1, 1 - b, k + b, 2 * i + 1)
                        if 4 <= i <= 4 + NEWTON_STEPS and ahead:
                            normalise(g + 1, 1 - b, i - 4, not start)
                        if i == 3 and not start:
                            keep_scores(g - 1, 1 - b)
                        if i == 0 and not (first and b == 0) and not (first and b == 1):
                            cut_lo(g - 2)

            for i in range(GROUP):
                measure(0, 0, 0, i)
            for part in range(NEWTON_STEPS + 1):
                normalise(0, 0, part, False)
            dve.wait_ge(w_loaded, 16 * (KC + 1))
            n = 0
            for k in range(KC):
                for a in range(2):
                    if n:
                        dve.wait_ge(wa_step, n)
                    nc.vector.scalar_tensor_tensor(out=scratch[:, :], in0=w_ext[:, k, 0:O], scalar=1.0,
                                                   in1=attn_bc[:, a, :], op0=ALU.mult, op1=ALU.mult,
                                                   accum_out=w_ext[:, k, O + a:O + a + 1]) \
                        .then_inc(wa_step, 1)
                    n += 1
            nc.vector.tensor_tensor(w_sq[:, :, :], w_ext[:, :, 0:O], w_ext[:, :, 0:O], ALU.mult) \
                .then_inc(wa_step, 1)
            rounds(dve, GROUPS // 2, two_groups)
            cut_lo(GROUPS - 2)
            keep_scores(GROUPS - 1, 1)

            dve.wait_ge(value_step, GROUPS * VALUE_STEPS)
            nc.vector.tensor_reduce(ext[:, 0:1], s_all[:, 1, :], op=ALU.max, axis=AX.X).then_inc(ext_step, 1)
            nc.vector.tensor_reduce(ext[:, 1:2], s_all[:, 1, :], op=ALU.min, axis=AX.X).then_inc(ext_step, 1)
            nc.vector.tensor_reduce(ext[:, 2:3], s_all[:, 0, :], op=ALU.min, axis=AX.X).then_inc(ext_step, 1)
            dve.wait_ge(norms_read, 2)
            nc.vector.tensor_scalar(ext[:, 4:5], ext[:, 4:5], -1.0, None, ALU.mult).then_inc(ext_step, 1)
            dve.wait_ge(ext_step, 4)
            nc.vector.tensor_scalar(ext[:, 1:3], ext[:, 1:3], -1.0, None, ALU.mult).then_inc(ext_ready, 1)
            dve.wait_ge(extT_done, 1)
            nc.vector.tensor_reduce(row_max[:, :], ps_ext[0:EXT, 0:PART], op=ALU.max, axis=AX.X) \
                .then_inc(ext_step, 1)
            dve.wait_ge(ext_step, 5)
            nc.vector.tensor_scalar(row_diag[:, :], ident[0:EXT, 0:EXT], row_max[:, 0:1], None, ALU.mult) \
                .then_inc(diag_ready, 1)
            dve.wait_ge(glob_done, 1)
            nc.vector.tensor_scalar(ur_bias[:, :], ps_ext[:, PART:PART + 1], SLOPE - 1.0,
                                    math.log(WEIGHT_SCALE), ALU.mult, ALU.add).then_inc(bias_ready, 1)
            nc.vector.tensor_copy(glob[:, :], ps_ext[:, PART:PART + EXT]).then_inc(glob_read, 1)

            def find_limits():
                dve.wait_ge(glob_read, 1)
                for i, limit in ((0, S2_LIMIT), (1, S2_LIMIT), (3, NORM_LIMIT), (4, -NORM_LEAST)):
                    nc.vector.tensor_scalar(over[:, i:i + 1], glob[:, i:i + 1], limit, None, ALU.is_le) \
                        .then_inc(over_step, 1)
                for i, a, b, op in ((2, 2, 0, ALU.subtract), (5, 1, 0, ALU.add)):
                    nc.vector.tensor_tensor(over[:, i:i + 1], glob[:, a:a + 1], glob[:, b:b + 1], op) \
                        .then_inc(over_step, 1)
                dve.wait_ge(over_step, 6)
                for i, limit in ((2, S1_LIMIT), (5, SPREAD_LIMIT)):
                    nc.vector.tensor_scalar(over[:, i:i + 1], over[:, i:i + 1], limit, None, ALU.is_le) \
                        .then_inc(over_step, 1)
                dve.wait_ge(over_step, 8)
                nc.vector.tensor_reduce(over[:, 0:1], over[:, :], op=ALU.min, axis=AX.X) \
                    .then_inc(over_step, 1)
                dve.wait_ge(over_step, 9)
                nc.vector.tensor_scalar(over_any[:, :], over[:, 0:1], -1.0, 1.0, ALU.mult, ALU.add) \
                    .then_inc(over_ready, 1)

            def weigh(q, c, start):
                s = STAGES * q + c
                if c == 0:
                    dve.wait_ge(r_loaded, 16 * q + 16)
                    if not start:
                        dve.wait_ge(p_ready, s)
                    nc.vector.tensor_copy(r_bc[:, :], r_in[:, :]).then_inc(r_ready, 1)
                    dve.wait_ge(r_ready, q + 1)
                dve.wait_ge(pT_done, s + 1)
                if not (start and c < RING):
                    dve.wait_ge(lo_ready, s - RING + 1)
                dve.nop(nofuse=True)
                for j in range(BLOCKS):
                    part = slice(j * WIDE, (j + 1) * WIDE)
                    last = nc.vector.scalar_tensor_tensor(
                        out=pT[c % RING][:, part], in0=r_bc[:, :], scalar=u_col[:, c * BLOCKS + j:c * BLOCKS + j + 1],
                        in1=ps_mask[c % RING][:, j, :], op0=ALU.max, op1=ALU.mult)
                last.then_inc(p_ready, 1)

            def cut_p(q, c):
                dve.wait_ge(hi_ready, STAGES * q + c + 1)
                nc.vector.scalar_tensor_tensor(out=pT_lo[:, c % RING, :], in0=pT[c % RING],
                                               scalar=0.0, in1=pT_hi[:, c % RING, :],
                                               op0=ALU.max, op1=ALU.subtract).then_inc(lo_ready, 1)

            EPI = 2

            def denominators(q):
                done = q * EPI
                for r in range(ROWS):
                    dve.wait_ge(acc_copied[r], q + 1)
                nc.vector.tensor_tensor(den[:, 0, :], acc_sb[:, :, O], acc_sb[:, :, O + 1], ALU.add) \
                    .then_inc(epi_step, 1)
                dve.wait_ge(epi_step, done + 1)
                nc.vector.tensor_scalar(den[:, 1, :], den[:, 0, :], 0.0, None, ALU.is_equal) \
                    .then_inc(flag_ready, 1)
                dve.wait_ge(flag_ready, q + 1)
                nc.vector.tensor_tensor(den[:, 2, :], den[:, 0, :], den[:, 1, :], ALU.add) \
                    .then_inc(epi_step, 1)
                dve.wait_ge(epi_step, done + 2)
                nc.vector.reciprocal(den[:, 3, :], den[:, 2, :]).then_inc(rden_ready, 1)

            def quad(q, first, last):
                for c in range(STAGES):
                    if c + 1 < STAGES:
                        weigh(q, c + 1, first)
                    elif not last:
                        weigh(q + 1, 0, False)
                    cut_p(q, c)
                    if not first:
                        if c == 3:
                            denominators(q - 1)

            dve.wait_ge(u_ready, 1)
            weigh(0, 0, True)
            cut_lo(GROUPS - 1)
            find_limits()
            rounds(dve, QUADS, quad)
            denominators(QUADS - 1)

            def general():
                STEPS = 3 * CHUNKS + 1

                def scores(t, c):
                    done = t * STEPS + 3 * c + 1
                    dve.wait_ge(g_step, done)
                    dve.wait_ge(g_adj_loaded, 16 * CHUNKS * t + 16 * c + 16)
                    nc.vector.tensor_scalar(edge.rearrange("p (m k n) -> p m k n", k=ROWS, n=PART),
                                            g_adj.rearrange("p (m n k) -> p m k n", k=ROWS, n=PART),
                                            0.0, 0.5, ALU.is_gt, ALU.subtract).then_inc(g_adj_read, 1)
                    part = slice(c * CHUNK, (c + 1) * CHUNK)
                    nc.vector.tensor_scalar(raw, s2_bc[:, part], s1_cur[:, 0:1], None, ALU.add) \
                        .then_inc(g_step, 1)
                    dve.wait_ge(g_step, done + 1)
                    nc.vector.scalar_tensor_tensor(out=leaky, in0=raw, scalar=SLOPE, in1=raw,
                                                   op0=ALU.mult, op1=ALU.max).then_inc(g_step, 1)
                    dve.wait_ge(g_step, done + 2)
                    dve.wait_ge(g_adj_read, CHUNKS * t + c + 1)
                    nc.vector.scalar_tensor_tensor(out=score[:, part], in0=edge, scalar=2 * MASKED,
                                                   in1=leaky, op0=ALU.mult, op1=ALU.min) \
                        .then_inc(g_step, 1)

                dve.wait_ge(g_s2T_done, 1)
                nc.vector.tensor_copy(s2T[:, :], ring[0][0:TILES, 0:PART]).then_inc(g_s2T_ready, 1)
                dve.wait_ge(g_s2_loaded, 16)
                with dve.Fori(0, TILES) as t:
                    nc.vector.tensor_copy(s1_cur[:, :], s_all[:, 0, bass.ds(t, 1)]).then_inc(g_step, 1)
                    for c in range(CHUNKS):
                        scores(t, c)
                    dve.wait_ge(g_step, t * STEPS + STEPS)
                    nc.vector.tensor_reduce(neg_max[:, 0:1], score, op=ALU.max, axis=AX.X) \
                        .then_inc(g_top_ready, 1)
                    dve.wait_ge(g_top_ready, t + 1)
                    nc.vector.tensor_scalar(neg_max[:, 1:2], neg_max[:, 0:1], -1.0, None, ALU.mult) \
                        .then_inc(g_max_ready, 1)
                    for n in range(FOUR):
                        dve.wait_ge(g_wT_done, FOUR * t + n + 1)
                        if n >= 2:
                            dve.wait_ge(g_summed, FOUR * t + n - 1)
                        nc.vector.tensor_copy(wT[:, n % 2, :], ring[n % 2][:, :]).then_inc(g_wT_ready, 1)
                    dve.wait_ge(g_w_ready, t + 1)
                    nc.vector.reciprocal(g_den[:, 1:2], g_den[:, 0:1]).then_inc(g_rden_ready, 1)
                    dve.wait_ge(g_rden_ready, t + 1)
                    dve.wait_ge(g_summed, FOUR * t + FOUR)
                    nc.vector.tensor_scalar(mean_part[:, 0:O], acc[0][:, 0:O], g_den[:, 1:2], None,
                                            ALU.mult).then_inc(g_y_ready, 1)
                    dve.wait_ge(g_y_ready, t + 1)
                    dve.wait_ge(g_x_loaded, 16 * t + 16)
                    nc.vector.scalar_tensor_tensor(out=x_quad[:, F:2 * F], in0=mean_part[:, 0:O],
                                                   scalar=0.0, in1=x_quad[:, 0:F],
                                                   op0=ALU.max, op1=ALU.add).then_inc(g_xp_ready, 1)
                    dve.wait_ge(g_xp_ready, t + 1)
                    dve.wait_ge(g_expm_ready, t + 1)
                    nc.vector.scalar_tensor_tensor(out=out_quad[:, 0:O], in0=neg_part[:, O:2 * O],
                                                   scalar=-1.0, in1=x_quad[:, F:2 * F],
                                                   op0=ALU.add, op1=ALU.add).then_inc(g_out_ready, 1)
                    dve.wait_ge(g_out_ready, t + 1)

            in_general(dve, general)

        @block.tensor
        def _(pe):
            def transpose_feat(g, i, start):
                n = g * GROUP + i
                pe.wait_ge(feat_ready, n + 1)
                if not (start and i < RING):
                    pe.wait_ge(featT_ready, n - RING + 1)
                for k in range(KC):
                    last = nc.tensor.transpose(ps_feat[i % RING][:, k * PART:(k + 1) * PART],
                                               feat[:, i % RING, k * PART:(k + 1) * PART], ident[:, :])
                last.then_inc(featT_done, 1)

            def h_product(g, i, start):
                n = g * GROUP + i
                pe.wait_ge(featT_ready, n + 1)
                if not (start and i < RING):
                    pe.wait_ge(h_ready, n - RING + 1)
                for k in range(KC):
                    last = nc.tensor.matmul(ps_h[i % RING], featT[:, i % RING, k * PART:(k + 1) * PART],
                                            w_ext[:, k, :], start=(k == 0), stop=(k == KC - 1))
                last.then_inc(h_done, 1)

            def two_groups(k, first, last):
                for b in range(2):
                    g = 2 * k + b
                    start = first and b == 0
                    for i in range(GROUP):
                        transpose_feat(g, i, start)
                        if i > 0:
                            h_product(g, i - 1, start)
                        elif not start:
                            h_product(g - 1, GROUP - 1, False)
                    if last and b == 1:
                        h_product(g, GROUP - 1, False)

            pe.wait_ge(const_ready, 4)
            pe.wait_ge(wa_step, 2 * KC + 1)
            for k in range(KC):
                last = nc.tensor.matmul(ps_norm, ones[:, :], w_sq[:, k, :], start=(k == 0), stop=(k == KC - 1))
            last.then_inc(norms_done, 1)
            rounds(pe, GROUPS // 2, two_groups)

            pe.wait_ge(ext_ready, 1)
            nc.tensor.transpose(ps_ext[0:EXT, 0:PART], ext[:, :], ident[:, :]).then_inc(extT_done, 1)
            nc.tensor.transpose(ps_s[0:TILES, 0:PART], s_all[:, 0, :], ident[:, :]).then_inc(sT_done, 1)
            pe.wait_ge(diag_ready, 1)
            nc.tensor.matmul(ps_ext[:, PART:PART + EXT], ones[0:EXT, :], row_diag[:, :],
                             start=True, stop=True).then_inc(glob_done, 1)
            pe.wait_ge(h_summed, GROUPS + 1)
            for i in range(GROUP):
                last = nc.tensor.matmul(ps_mean[:, 0:O], ones[:, :], h_sum[:, i, :],
                                        start=(i == 0), stop=(i == GROUP - 1))
            last.then_inc(mean_done, 1)

            def transpose_mask(q, c, start):
                s = STAGES * q + c
                if c % PER_PIECE == 0:
                    pe.wait_ge(mask_ready, PIECES * q + c // PER_PIECE + 1)
                if not (start and c < RING):
                    pe.wait_ge(p_ready, s - RING + 1)
                for r in range(ROWS):
                    last = nc.tensor.transpose(ps_pairs[c % RING][:, r * PART:(r + 1) * PART],
                                               mask_pairs[:, c // PER_PIECE % RING, r, c % PER_PIECE, :],
                                               ident_bf[:, :])
                last.then_inc(pT_done, 1)

            def add_hi(c, j, r):
                node = c * BLOCKS + j
                w = pT_hi[:, c % RING, j * WIDE + r * PART:j * WIDE + (r + 1) * PART]
                nc.tensor.matmul(acc[r][:, 0:O + 2], w, value_hi[:, node, :], start=(node == 0), stop=False)
                nc.tensor.matmul(acc[r][:, 0:O], w, value_lo[:, node, :], start=False, stop=False)

            def add_lo(c, j, r):
                node = c * BLOCKS + j
                w = pT_lo[:, c % RING, j * WIDE + r * PART:j * WIDE + (r + 1) * PART]
                return nc.tensor.matmul(acc[r][:, 0:O + 1], w, value_hi[:, node, 0:O + 1],
                                        start=False, stop=(node == TILES - 1))

            def quad(q, first, last):
                for c in range(STAGES):
                    s = STAGES * q + c
                    pe.wait_ge(hi_ready, s + 1)
                    if first and c == STAGES - GROUP // BLOCKS:
                        pe.wait_ge(lo_cut, GROUPS)
                    if c < STAGES - 1:
                        for r in range(ROWS):
                            if c == 0 and not first:
                                pe.wait_ge(acc_copied[r], q)
                            for j in range(BLOCKS):
                                add_hi(c, j, r)
                    if c + AHEAD < STAGES:
                        transpose_mask(q, c + AHEAD, first)
                    elif not last:
                        transpose_mask(q + 1, c + AHEAD - STAGES, False)
                    pe.wait_ge(lo_ready, s + 1)
                    if c < STAGES - 1:
                        for r in range(ROWS):
                            for j in range(BLOCKS):
                                end = add_lo(c, j, r)
                        end.then_inc(stage_summed, 1)
                    else:
                        for r in range(ROWS):
                            for j in range(BLOCKS):
                                add_hi(c, j, r)
                            for j in range(BLOCKS):
                                end = add_lo(c, j, r)
                            end.then_inc(row_summed if r < ROWS - 1 else stage_summed, 1)

            pe.wait_ge(mean_ready, 1)
            pe.wait_ge(rT_ready, 1)
            pe.wait_ge(glob_read, 1)
            for c in range(AHEAD):
                transpose_mask(0, c, True)
            pe.wait_ge(lo_cut, GROUPS - 1)
            rounds(pe, QUADS, quad)

            def general():
                pe.wait_ge(g_h_loaded, 16)
                nc.tensor.transpose(ring[0][0:TILES, 0:PART], s_all[:, 1, :], ident[:, :]) \
                    .then_inc(g_s2T_done, 1)

                def transpose_w(t, n):
                    if n >= 2:
                        pe.wait_ge(g_wT_ready, FOUR * t + n - 1)
                    for j in range(4):
                        at = (4 * n + j) * PART
                        last = nc.tensor.transpose(ring[n % 2][:, j * PART:(j + 1) * PART],
                                                   score[:, at:at + PART], ident[:, :])
                    last.then_inc(g_wT_done, 1)

                with pe.Fori(0, TILES) as t:
                    pe.wait_ge(g_w_ready, t + 1)
                    transpose_w(t, 0)
                    for n in range(FOUR):
                        if n + 1 < FOUR:
                            transpose_w(t, n + 1)
                        pe.wait_ge(g_wT_ready, FOUR * t + n + 1)
                        for j in range(4):
                            node = 4 * n + j
                            last = nc.tensor.matmul(acc[0][:, 0:O], wT[:, n % 2, j * PART:(j + 1) * PART],
                                                    h_all[:, node, :], start=(node == 0),
                                                    stop=(node == TILES - 1))
                        last.then_inc(g_summed, 1)

            in_general(pe, general)


_INS = ['x', 'adj', 'L0_gnn_W', 'L0_gnn_attn']


def kernel(**inputs):
    import numpy as _np
    import concourse.bacc as _bacc
    from concourse import mybir as _mybir
    from concourse.bass_utils import run_bass_kernel_spmd as _run

    nc = _bacc.Bacc("TRN2", target_bir_lowering=False, num_devices=1)
    arrays, args = {}, []
    for name in _INS:
        a = _np.ascontiguousarray(inputs[name])
        arrays[f"in_{name}_dram"] = a
        args.append(nc.dram_tensor(f"in_{name}_dram", a.shape, _mybir.dt.from_np(a.dtype), kind="ExternalInput").ap())
    x = arrays["in_x_dram"]
    args.append(nc.dram_tensor("out_dram", x.shape, _mybir.dt.from_np(x.dtype), kind="ExternalOutput").ap())
    gat_kernel(nc, *args)
    r = _run(nc, [arrays], core_ids=[0])
    return r.results[0]["out_dram"]
```

```python
import concourse.bass as bass
from concourse import mybir
from contextlib import ExitStack
import math

FP32 = mybir.dt.float32
FP16 = mybir.dt.float16
FP8 = mybir.dt.float8e4
BF16 = mybir.dt.bfloat16
I32 = mybir.dt.int32
ALU = mybir.AluOpType
ACT = mybir.ActivationFunctionType
AX = mybir.AxisListType

PART = 128
SLOPE = 0.2
LN_EPS = 1e-5
VALUE_SCALE = 256.0
WEIGHT_SCALE = 1024.0
S2_LIMIT = 10.0
S1_LIMIT = 5.0
SPREAD_LIMIT = 9.0
NORM_LIMIT = 4.5
NORM_LEAST = 1.0 / 256
MASKED = 9e15
RSQRT_SEED = float(0x5F3759DF)
NEWTON_STEPS = 3


def gat_kernel(nc, x, adj, W, attn, out):
    N, F = x.shape
    O = W.shape[1]
    TILES = N // PART
    GROUP = 8
    GROUPS = TILES // GROUP
    CUTS = 2
    KC = F // PART
    HC = O + 2
    RING = 4
    ROWS = 4
    QUADS = TILES // ROWS
    WIDE = ROWS * PART
    PIECE = 512
    PIECES = N // PIECE
    BLOCKS = 2
    STAGES = TILES // BLOCKS
    PER_PIECE = PIECE // (BLOCKS * PART)
    VALUE_STEPS = 4
    LEAD = 2
    AHEAD = 4

    x_tiles = x.rearrange("(m p k) f -> p m (k f)", p=PART, k=ROWS)
    adj_tiles = adj.rearrange("(m p k) n -> p m k n", p=PART, k=ROWS)
    out_tiles = out.rearrange("(m p k) f -> p m (k f)", p=PART, k=ROWS)
    attn_rows = attn.rearrange("(two n) one -> one two n", two=2)

    CHUNK = 2048
    CHUNKS = N // CHUNK
    FOUR = TILES // 4

    h_dram = nc.dram_tensor("h_all", [PART, TILES, O], FP32).ap()
    s2_dram = nc.dram_tensor("s2_row", [TILES, PART], FP32).ap()
    r_dram = nc.dram_tensor("r_row", [TILES, PART], FP32).ap()

    ctx = ExitStack()
    with ctx:
        def sb(name, shape, dt):
            return ctx.enter_context(nc.sbuf_tensor(name, shape, dt))

        def sem(name):
            return ctx.enter_context(nc.semaphore(name))

        ident = sb("ident", [PART, PART], FP32)
        ident_bf = sb("ident_bf", [PART, PART], BF16)
        ones = sb("ones", [PART, PART], FP32)
        minus_half = sb("minus_half", [PART, 1], FP32)
        w_ext = sb("w_ext", [PART, KC, HC], FP32)
        s_all = sb("s_all", [PART, 2, TILES], FP32)
        u_col = sb("u_col", [PART, TILES], FP32)
        EXT = 5
        ext = sb("ext", [PART, EXT], FP32)
        top = sb("top", [1, 1], FP32)
        row_max = sb("row_max", [EXT, 1], FP32)
        row_diag = sb("row_diag", [EXT, EXT], FP32)
        glob = sb("glob", [PART, EXT], FP32)
        kept = sb("kept", [PART, 6], FP32)
        within = sb("within", [PART, 1], FP32)
        all_within = sb("all_within", [PART, 1], FP32)
        over_any = sb("over_any", [PART, 1], I32)
        w_sq = sb("w_sq", [PART, KC, O], FP32)
        ur_bias = sb("ur_bias", [PART, 1], FP32)
        rT = sb("rT", [TILES, PART], FP32)
        values = sb("values", [PART, TILES * (2 * O + 2)], FP16)
        value_lo = values[:, 0:TILES * O].rearrange("p (t f) -> p t f", t=TILES)
        value_hi = values[:, TILES * O:].rearrange("p (t f) -> p t f", t=TILES)

        arena = sb("arena", [PART, TILES * F], FP32)
        x_in = arena[:, :].rearrange("p (t f) -> p t f", t=TILES)
        ADJ = RING * ROWS * PIECE
        MASK = ADJ // 4
        CUT = RING * BLOCKS * WIDE // 2
        adj_in = arena[:, 0:ADJ].bitcast(I32).rearrange("p (b r c) -> p b r c", b=RING, r=ROWS)
        mask = arena[:, ADJ:ADJ + MASK].bitcast(FP8).rearrange("p (b r c) -> p b r c", b=RING, r=ROWS)
        mask_pairs = arena[:, ADJ:ADJ + MASK].bitcast(BF16).rearrange(
            "p (b r c two) -> p b r two c", b=RING, r=ROWS, two=PER_PIECE)
        pT_hi = arena[:, ADJ + MASK:ADJ + MASK + CUT].bitcast(FP16).rearrange("p (b w) -> p b w", b=RING)
        pT_lo = arena[:, ADJ + MASK + CUT:ADJ + MASK + 2 * CUT].bitcast(FP16) \
            .rearrange("p (b w) -> p b w", b=RING)

        arena2 = sb("arena2", [PART, 2 * GROUP * (HC + O)], FP32)
        H = 2 * GROUP * HC
        h_buf = arena2[:, 0:H].rearrange("p (b t f) -> p b t f", b=2, t=GROUP)
        scaled_h = arena2[:, H:H + 2 * GROUP * O].rearrange("p (b t f) -> p b t f", b=2, t=GROUP)
        HALF = 2 * BLOCKS * WIDE
        Q = ROWS * O
        at = HALF
        acc_sb = arena2[:, at:at + ROWS * (O + 2)].rearrange("p (r f) -> p r f", r=ROWS)
        at += ROWS * (O + 2)
        y = arena2[:, at:at + Q]
        expm = arena2[:, at + Q:at + 2 * Q]
        x_plus = arena2[:, at + 2 * Q:at + 3 * Q]
        elu_neg = arena[:, ADJ + MASK + 2 * CUT:ADJ + MASK + 2 * CUT + Q]

        arena3 = sb("arena3", [PART, 2 * RING * F], FP32)
        feat = arena3[:, 0:RING * F].rearrange("p (b f) -> p b f", b=RING)
        featT = arena3[:, RING * F:2 * RING * F].rearrange("p (b f) -> p b f", b=RING)
        pT = [half[:, i * BLOCKS * WIDE:(i + 1) * BLOCKS * WIDE] for half in (arena2, arena3) for i in range(2)]

        r_in = sb("r_in", [PART, WIDE], FP32)
        s1_diag = r_in[:, :].rearrange("p (r n) -> p r n", r=ROWS)
        r_bc = sb("r_bc", [PART, WIDE], FP32)
        x_quad = sb("x_quad", [PART, Q], FP32)
        pos_part = sb("pos_part", [PART, Q], FP32)
        neg_part = sb("neg_part", [PART, Q], FP32)
        out_quad = sb("out_quad", [PART, Q], FP32)
        g_y = sb("g_y", [PART, Q], FP32)
        den = sb("den", [PART, 2, ROWS], FP32)
        least_den = sb("least_den", [PART, ROWS], FP32)

        h_all = values[:, 0:TILES * 2 * O].bitcast(FP32).rearrange("p (t f) -> p t f", t=TILES)
        s2_bc = arena[:, 0:N]
        score = arena[:, N:2 * N]
        g_adj = arena2[:, 0:CHUNK].bitcast(I32)
        edge = arena2[:, CHUNK:2 * CHUNK]
        raw = arena2[:, 2 * CHUNK:3 * CHUNK]
        leaky = arena2[:, 3 * CHUNK:4 * CHUNK]
        wT = arena3[:, 0:2 * 4 * PART].rearrange("p (b w) -> p b w", b=2)
        s2T = sb("s2T", [TILES, PART], FP32)
        s1_cur = sb("s1_cur", [PART, 1], FP32)
        neg_max = sb("neg_max", [PART, 2], FP32)
        g_den = sb("g_den", [PART, 2], FP32)

        attn_bc = sb("attn_bc", [PART, 2, O], FP32)
        scratch = sb("scratch", [PART, O], FP32)
        stats = sb("stats", [PART, GROUP, 6], FP32)
        mean_var = sb("mean_var", [PART, GROUP, 2], FP32)
        var_eps = sb("var_eps", [PART, GROUP], FP32)
        seed = sb("seed", [PART, GROUP], I32)
        newton = sb("newton", [PART, GROUP], FP32)
        rstd = sb("rstd", [PART, 2, GROUP], FP32)
        shift = sb("shift", [PART, 2, GROUP], FP32)
        d_col = sb("d_col", [PART, 2, GROUP], FP32)
        d_scaled = sb("d_scaled", [PART, 2, GROUP], FP32)

        ring = [ctx.enter_context(nc.psum_tensor(f"ring{i}", [PART, 512], FP32)) for i in range(RING)]
        acc = [ctx.enter_context(nc.psum_tensor(f"acc{i}", [PART, 512], FP32)) for i in range(ROWS)]
        ps_pairs = [ring[i][:, :].bitcast(BF16)[:, 0:WIDE] for i in range(RING)]
        ps_mask = [ring[i][:, 0:WIDE // 2].bitcast(FP8).rearrange("p (w two) -> p two w", two=BLOCKS)
                   for i in range(RING)]
        ps_feat = [ring[i][:, 0:F] for i in range(RING)]
        ps_h = [acc[i][:, 0:HC] for i in range(RING)]
        ps_norm = ring[RING - 1][:, F:F + O]
        ps_top, ps_s, ps_s1, ps_ext = acc
        ps_within = ring[0][:, 0:1]

        w_loaded = sem("w_loaded")
        const_ready = sem("const_ready")
        w_sq_ready = sem("w_sq_ready")
        wa_step = sem("wa_step")
        x_first = sem("x_first")
        x_loaded = [sem("x_loaded0"), sem("x_loaded1")]
        norm_step = sem("norm_step")
        norm_ready = sem("norm_ready")
        feat_ready = sem("feat_ready")
        featT_done = sem("featT_done")
        featT_ready = sem("featT_ready")
        h_done = sem("h_done")
        h_ready = sem("h_ready")
        d_ready = sem("d_ready")
        value_step = sem("value_step")
        scaled_ready = sem("scaled_ready")
        hi_cut = sem("hi_cut")
        lo_cut = sem("lo_cut")
        top_ready = sem("top_ready")
        topT_done = sem("topT_done")
        top_row_ready = sem("top_row_ready")
        top_done = sem("top_done")
        s1_diag_ready = sem("s1_diag_ready")
        s1_done = sem("s1_done")
        ext_ready = sem("ext_ready")
        ext_step = sem("ext_step")
        extT_done = sem("extT_done")
        sT_done = sem("sT_done")
        diag_ready = sem("diag_ready")
        glob_done = sem("glob_done")
        bias_ready = sem("bias_ready")
        rT_ready = sem("rT_ready")
        u_ready = sem("u_ready")
        r_stored = sem("r_stored")

        h_stored = [sem("h_stored0"), sem("h_stored1")]
        norms_done = sem("norms_done")
        norms_read = sem("norms_read")
        glob_read = sem("glob_read")
        over_step = sem("over_step")
        over_ready = sem("over_ready")
        within_ready = sem("within_ready")
        within_summed = sem("within_summed")

        g_h_loaded = sem("g_h_loaded")
        g_s2T_done = sem("g_s2T_done")
        g_s2T_ready = sem("g_s2T_ready")
        g_s2_stored = sem("g_s2_stored")
        g_s2_loaded = sem("g_s2_loaded")
        g_x_loaded = sem("g_x_loaded")
        g_adj_loaded = sem("g_adj_loaded")
        g_adj_read = sem("g_adj_read")
        g_step = sem("g_step")
        g_top_ready = sem("g_top_ready")
        g_max_ready = sem("g_max_ready")
        g_w_ready = sem("g_w_ready")
        g_wT_done = sem("g_wT_done")
        g_wT_ready = sem("g_wT_ready")
        g_summed = sem("g_summed")
        g_rden_ready = sem("g_rden_ready")
        g_y_ready = sem("g_y_ready")
        g_neg_ready = sem("g_neg_ready")
        g_expm_ready = sem("g_expm_ready")
        g_xp_ready = sem("g_xp_ready")
        g_out_ready = sem("g_out_ready")
        g_out_stored = sem("g_out_stored")

        adj_loaded = [sem(f"adj_loaded{i}") for i in range(RING)]
        r_loaded = sem("r_loaded")
        r_ready = sem("r_ready")
        mask_ready = sem("mask_ready")
        pT_done = sem("pT_done")
        p_ready = sem("p_ready")
        hi_ready = sem("hi_ready")
        lo_ready = sem("lo_ready")
        stage_summed = sem("stage_summed")
        row_summed = sem("row_summed")
        acc_copied = [sem(f"acc_copied{r}") for r in range(ROWS)]
        den_ready = sem("den_ready")
        least_ready = sem("least_ready")
        rden_ready = sem("rden_ready")
        pos_ready = sem("pos_ready")
        elu_ready = sem("elu_ready")
        y_ready = sem("y_ready")
        neg_ready = sem("neg_ready")
        expm_ready = sem("expm_ready")
        xp_ready = sem("xp_ready")
        out_ready = sem("out_ready")
        x_back = sem("x_back")
        out_stored = sem("out_stored")

        block = ctx.enter_context(nc.Block())

        def rounds(eng, count, one):
            one(0, True, False)
            with eng.Fori(1, count - 1) as k:
                one(k, False, False)
            one(count - 1, False, True)

        def in_general(eng, general):
            eng.wait_ge(over_ready, 1)
            with eng.If(eng.value_load(over_any[0:1, 0:1], min_val=0, max_val=1) != 0):
                general()

        @block.sync
        def _(sync):
            def load_x(k, b):
                sync.dma_start(x_in[:, bass.ts(2 * k + b, GROUP), :]
                               .rearrange("p (m k) f -> p m (k f)", k=ROWS),
                               x_tiles[:, bass.ts(2 * k + b, GROUP // ROWS), :]).then_inc(x_loaded[b], 16)

            def load_adj(q, e):
                sync.dma_start(adj_in[:, e % RING, :, :],
                               adj_tiles[:, bass.ds(q, 1), :, e * PIECE:(e + 1) * PIECE]
                               .rearrange("p m k c -> p (m k) c")) \
                    .then_inc(adj_loaded[e % RING], 16)

            sync.dma_start(x_in[:, 0:ROWS, :].rearrange("p k f -> p (k f)"), x_tiles[:, 0, :]).then_inc(x_first, 16)
            sync.dma_start(x_in[:, ROWS:GROUP, :].rearrange("p k f -> p (k f)"), x_tiles[:, 1, :]) \
                .then_inc(x_loaded[0], 16)
            for k in range(KC):
                sync.dma_start(w_ext[:, k, 0:O], W[k * PART:(k + 1) * PART, :]).then_inc(w_loaded, 16)
            sync.dma_start(attn_bc[:, :, :], attn_rows.to_broadcast([PART, 2, O])).then_inc(w_loaded, 16)
            load_x(0, 1)

            def store_h(k):
                for b in range(2):
                    g = 2 * k + b
                    sync.wait_ge(h_ready, (g + 1) * GROUP)
                    sync.dma_start(h_dram[:, bass.ts(g, GROUP), :], h_buf[:, b, :, 0:O]) \
                        .then_inc(h_stored[b], 16)

            with sync.Fori(1, GROUPS // 2) as k:
                for b in range(2):
                    sync.wait_ge(x_loaded[b], 16 * k)
                    load_x(k, b)
                store_h(k - 1)

            sync.wait_ge(feat_ready, TILES // 2)
            for e in range(RING):
                load_adj(0, e)
            store_h(GROUPS // 2 - 1)

            sync.wait_ge(rT_ready, 1)
            sync.dma_start(r_dram, rT[:, :]).then_inc(r_stored, 16)
            sync.wait_ge(r_stored, 16)
            r_rows = r_dram.rearrange("(q r) p -> q (r p)", r=ROWS)

            def quad(q, first, last):
                if not last:
                    sync.wait_ge(r_ready, q + 1)
                    sync.dma_start(r_in[:, :], r_rows[bass.ds(q + 1, 1), :].to_broadcast([PART, WIDE])) \
                        .then_inc(r_loaded, 16)
                for e in range(PIECES):
                    if e + RING < PIECES:
                        sync.wait_ge(mask_ready, 2 * (PIECES * q + e + 1))
                        load_adj(q, e + RING)
                    elif not last:
                        sync.wait_ge(mask_ready, 2 * (PIECES * q + e + 1))
                        load_adj(q + 1, e + RING - PIECES)
                    if e == 7:
                        if not first:
                            sync.wait_ge(out_ready, q)
                            sync.dma_start(out_tiles[:, bass.ds(q - 1, 1), :],
                                           out_quad[:, :].rearrange("p (m f) -> p m f", m=1)) \
                                .then_inc(out_stored, 16)
                            sync.wait_ge(xp_ready, q)
                        sync.dma_start(x_quad[:, :].rearrange("p (m f) -> p m f", m=1),
                                       x_tiles[:, bass.ds(q, 1), :]).then_inc(x_back, 16)

            rounds(sync, QUADS, quad)
            sync.wait_ge(out_ready, QUADS)
            sync.dma_start(out_tiles[:, QUADS - 1, :], out_quad[:, :]).then_inc(out_stored, 16)
            sync.wait_ge(out_stored, 16 * QUADS + 16)

            x_rows, adj_rows, out_rows = (a.rearrange("(m p k) n -> m k p n", p=PART, k=ROWS)
                                          for a in (x, adj, out))

            def tile_in_general(m, k):
                t = ROWS * m + k
                sync.dma_start(x_quad[:, 0:F], x_rows[bass.ds(m, 1), k, :, :].rearrange("m p f -> (m p) f")) \
                    .then_inc(g_x_loaded, 16)
                for c in range(CHUNKS):
                    if c > 0:
                        sync.wait_ge(g_adj_read, CHUNKS * t + c)
                    sync.dma_start(g_adj, adj_rows[bass.ds(m, 1), k, :, c * CHUNK:(c + 1) * CHUNK]
                                   .rearrange("m p n -> (m p) n")).then_inc(g_adj_loaded, 16)
                sync.wait_ge(g_out_ready, t + 1)
                sync.dma_start(out_rows[bass.ds(m, 1), k, :, :].rearrange("m p f -> (m p) f"),
                               out_quad[:, 0:O]).then_inc(g_out_stored, 16)
                sync.wait_ge(g_out_stored, 16 * t + 16)
                sync.nop(nofuse=True)

            def general():
                for b in range(2):
                    sync.wait_ge(h_stored[b], 16 * (GROUPS // 2))
                sync.dma_start(h_all, h_dram).then_inc(g_h_loaded, 16)
                sync.wait_ge(g_s2T_ready, 1)
                sync.dma_start(s2_dram, s2T[:, :]).then_inc(g_s2_stored, 16)
                sync.wait_ge(g_s2_stored, 16)
                s2_row = s2_dram.rearrange("(one t) p -> one (t p)", one=1)
                sync.dma_start(s2_bc, s2_row.to_broadcast([PART, N])).then_inc(g_s2_loaded, 16)
                with sync.Fori(0, QUADS) as m:
                    for k in range(ROWS):
                        tile_in_general(m, k)

            in_general(sync, general)

        @block.gpsimd
        def _(pool):
            pool.memset(ones[:, :], 1.0).then_inc(const_ready, 1)
            pool.memset(ident[:, :], 0.0).then_inc(const_ready, 1)
            pool.wait_ge(const_ready, 2)
            pool.affine_select(out=ident[:, :], in_=ident[:, :], compare_op=ALU.not_equal, fill=1.0,
                               base=0, pattern=[[-1, PART]], channel_multiplier=1).then_inc(const_ready, 1)
            pool.wait_ge(const_ready, 3)
            pool.tensor_copy(ident_bf[:, :], ident[:, :]).then_inc(const_ready, 1)
            pool.memset(minus_half[:, :], -0.5).then_inc(const_ready, 1)
            pool.memset(least_den[:, :], 1.0).then_inc(least_ready, 1)
            pool.memset(out_quad[:, :], 0.0).then_inc(out_stored, 16)
            pool.wait_ge(w_loaded, 16 * (KC + 1))
            nc.gpsimd.tensor_tensor(w_sq[:, :, :], w_ext[:, :, 0:O], w_ext[:, :, 0:O], ALU.mult) \
                .then_inc(w_sq_ready, 1)

            def cut_lo(g, b):
                pool.wait_ge(hi_cut, CUTS * (g + 1))
                nc.gpsimd.tensor_tensor(value_lo[:, bass.ts(g, GROUP), :], scaled_h[:, b, :, :],
                                        value_hi[:, bass.ts(g, GROUP), 0:O], ALU.subtract) \
                    .then_inc(lo_cut, 1)

            def two_groups(k, first, last):
                for b in range(2):
                    g = 2 * k + b
                    pool.wait_ge(value_step, g * VALUE_STEPS + 2)
                    if not first:
                        pool.wait_ge(lo_cut, g - 1)
                    nc.gpsimd.tensor_tensor(scaled_h[:, b, :, :], h_buf[:, b, :, 0:O],
                                            d_scaled[:, b, :].unsqueeze(2).to_broadcast([PART, GROUP, O]),
                                            ALU.mult).then_inc(scaled_ready, 1)
                    if not (first and b == 0):
                        cut_lo(g - 1, 1 - b)

            rounds(pool, GROUPS // 2, two_groups)
            cut_lo(GROUPS - 1, 1)

            with pool.Fori(0, QUADS - 1) as q:
                pool.wait_ge(pos_ready, q + 1)
                pool.wait_ge(x_back, 16 * q + 16)
                nc.gpsimd.tensor_tensor(x_plus, pos_part[:, :], x_quad[:, :], ALU.add).then_inc(xp_ready, 1)
                pool.wait_ge(expm_ready, q + 1)
                pool.nop(nofuse=True)
                nc.gpsimd.tensor_scalar(elu_neg, expm, -1.0, 1.0, ALU.add, ALU.mult).then_inc(elu_ready, 1)
                pool.wait_ge(elu_ready, q + 1)
                pool.wait_ge(xp_ready, q + 1)
                pool.wait_ge(out_stored, 16 * q + 16)
                nc.gpsimd.tensor_tensor(out_quad[:, :], elu_neg, x_plus, ALU.add).then_inc(out_ready, 1)

        @block.scalar
        def _(act):
            CUT_AT = (3, 7)
            LAG = 3

            def h_out(g, b, i, first, pair_no):
                act.wait_ge(h_done, g * GROUP + i + 1)
                if i == 0 and not first:
                    act.wait_ge(scaled_ready, g - 1)
                    act.wait_ge(value_step, (g - 1) * VALUE_STEPS)
                    act.wait_ge(h_stored[b], 16 * pair_no)
                nc.scalar.activation(h_buf[:, b, i, :], ps_h[i % RING], ACT.Copy).then_inc(h_ready, 1)

            def make_d(g, b):
                act.wait_ge(h_ready, (g + 1) * GROUP)
                nc.scalar.activation(d_col[:, b, :], h_buf[:, b, :, O + 1], ACT.Exp, scale=SLOPE) \
                    .then_inc(d_ready, 1)

            def cut_hi(g, b, part):
                act.wait_ge(scaled_ready, g + 1)
                n = GROUP // CUTS
                nc.scalar.activation(value_hi[:, bass.ts(g * CUTS + part, n), 0:O],
                                     scaled_h[:, b, part * n:(part + 1) * n, :], ACT.Copy) \
                    .then_inc(hi_cut, 1)

            def two_groups(k, first, last):
                for b in range(2):
                    g = 2 * k + b
                    start = first and b == 0
                    for i in range(GROUP):
                        if i == 0:
                            act.wait_ge(norm_ready, g + 1)
                        if not (start and i < RING):
                            act.wait_ge(featT_done, g * GROUP + i - RING + 1)
                        nc.scalar.activation(feat[:, i % RING, :], x_in[:, g * GROUP + i, :], ACT.Relu,
                                             bias=shift[:, b, i:i + 1], scale=rstd[:, b, i:i + 1]) \
                            .then_inc(feat_ready, 1)
                        if i >= LAG:
                            h_out(g, b, i - LAG, first, k)
                        elif not start:
                            h_out(g - 1, 1 - b, i - LAG + GROUP, first, k)
                        if i == LAG - 1 and not start:
                            make_d(g - 1, 1 - b)
                        if i in CUT_AT and not first:
                            cut_hi(g - 2, b, CUT_AT.index(i))
                    if last and b == 1:
                        for i in range(GROUP - LAG, GROUP):
                            h_out(g, b, i, first, k)
                        make_d(g, b)

            rounds(act, GROUPS // 2, two_groups)

            def make_mask(q, e, half, start):
                act.wait_ge(adj_loaded[e % RING], 16 * (PIECES // RING) * q + 16 * (e // RING) + 16)
                if not (start and e < RING):
                    act.wait_ge(pT_done, PER_PIECE * (PIECES * q + e - RING + 1))
                act.nop(nofuse=True)
                rows = slice(half * ROWS // 2, (half + 1) * ROWS // 2)
                nc.scalar.activation(mask[:, e % RING, rows, :], adj_in[:, e % RING, rows, :], ACT.Sign,
                                     bias=minus_half[:, 0:1], saturate=False) \
                    .then_inc(mask_ready, 1)

            act.wait_ge(const_ready, 5)
            for half in range(2):
                make_mask(0, 0, half, True)

            act.wait_ge(s1_done, 1)
            act.wait_ge(bias_ready, 1)
            nc.scalar.activation(r_bc[:, :], ps_s1[:, 0:WIDE], ACT.Exp, bias=ur_bias[:, 0:1],
                                 scale=SLOPE - 1.0).then_inc(r_ready, 1)
            nc.scalar.activation(u_col[:, :], s_all[:, 1, :], ACT.Exp, bias=ur_bias[:, 0:1],
                                 scale=1.0 - SLOPE).then_inc(u_ready, 1)
            act.wait_ge(sT_done, 1)
            nc.scalar.activation(rT[:, :], ps_s[0:TILES, 0:PART], ACT.Exp, bias=ur_bias[0:TILES, 0:1],
                                 scale=SLOPE - 1.0).then_inc(rT_ready, 1)
            for half in range(2):
                make_mask(0, 1, half, True)

            def copy_acc(q, r):
                if r < ROWS - 1:
                    act.wait_ge(row_summed, (ROWS - 1) * q + r + 1)
                else:
                    act.wait_ge(stage_summed, STAGES * q + STAGES)
                nc.scalar.activation(acc_sb[:, r, :], acc[r][:, 0:O + 2], ACT.Copy) \
                    .then_inc(acc_copied[r], 1)

            def rows_y(q):
                act.wait_ge(rden_ready, q + 1)
                for r in range(ROWS):
                    last = nc.scalar.activation(y[:, r * O:(r + 1) * O], acc_sb[:, r, 0:O], ACT.Copy,
                                                scale=den[:, 1, r:r + 1])
                last.then_inc(y_ready, 1)

            def elu_exp(q, last=False):
                act.wait_ge(y_ready, q + 1)
                nc.scalar.activation(neg_part[:, :], y, ACT.Relu, scale=-1.0).then_inc(neg_ready, 1)
                act.wait_ge(neg_ready, q + 1)
                nc.scalar.activation(expm, neg_part[:, :], ACT.Exp, scale=-1.0).then_inc(expm_ready, 1)
                if not last:
                    nc.scalar.activation(pos_part[:, :], y, ACT.Relu).then_inc(pos_ready, 1)

            def quad(q, first, last):
                for c in range(STAGES):
                    s = STAGES * q + c
                    act.wait_ge(p_ready, s + 1)
                    if not (first and c < RING):
                        act.wait_ge(stage_summed, s - RING + 1)
                    nc.scalar.activation(pT_hi[:, c % RING, :], pT[c % RING], ACT.Relu) \
                        .then_inc(hi_ready, 1)
                    if c == 0 and first:
                        for half in range(2):
                            make_mask(0, 2, half, True)
                    if c == 2 and first:
                        for part in range(CUTS):
                            cut_hi(GROUPS - 2, 0, part)
                    if c == 4 and first:
                        for part in range(CUTS):
                            cut_hi(GROUPS - 1, 1, part)
                        act.wait_ge(h_stored[1], 16 * (GROUPS // 2))
                    if c == 1 and not first:
                        for r in range(ROWS):
                            copy_acc(q - 1, r)
                    if c == 5 and not first:
                        rows_y(q - 1)
                    e = c // PER_PIECE + RING - 1
                    if e < PIECES:
                        make_mask(q, e, c % PER_PIECE, first)
                    elif not last:
                        make_mask(q + 1, e - PIECES, c % PER_PIECE, False)
                    if c == 11 and not first:
                        elu_exp(q - 1)

            rounds(act, QUADS, quad)
            for r in range(ROWS):
                copy_acc(QUADS - 1, r)
            rows_y(QUADS - 1)
            elu_exp(QUADS - 1, True)

            def general():
                with act.Fori(0, TILES) as t:
                    act.wait_ge(g_max_ready, t + 1)
                    nc.scalar.activation(score, score, ACT.Exp, bias=neg_max[:, 1:2],
                                         accum_out=g_den[:, 0:1]).then_inc(g_w_ready, 1)
                    act.wait_ge(g_y_ready, t + 1)
                    nc.scalar.activation(neg_part[:, 0:O], g_y[:, 0:O], ACT.Relu, scale=-1.0) \
                        .then_inc(g_neg_ready, 1)
                    act.wait_ge(g_neg_ready, t + 1)
                    nc.scalar.activation(neg_part[:, O:2 * O], neg_part[:, 0:O], ACT.Exp, scale=-1.0) \
                        .then_inc(g_expm_ready, 1)

            in_general(act, general)

        @block.vector
        def _(dve):
            NORM = GROUP + 4 + 3 * NEWTON_STEPS

            def measure(g, b, k, i):
                if i == 0:
                    dve.wait_ge(x_loaded[b], 16 * k + 16)
                nc.vector.bn_stats(stats[:, i, :], x_in[:, g * GROUP + i, :]).then_inc(norm_step, 1)

            def normalise(g, b, part, has_before):
                done = g * NORM
                if part == 0:
                    dve.wait_ge(norm_step, done + GROUP)
                    dve.nop(nofuse=True)
                    for i in range(GROUP):
                        last = nc.vector.bn_aggr(mean_var[:, i, :], stats[:, i, :])
                    last.then_inc(norm_step, 1)
                    dve.wait_ge(norm_step, done + GROUP + 1)
                    nc.vector.tensor_scalar(var_eps[:, :], mean_var[:, :, 1], LN_EPS, None, ALU.add) \
                        .then_inc(norm_step, 1)
                    dve.wait_ge(norm_step, done + GROUP + 2)
                    nc.vector.tensor_scalar(seed[:, :], var_eps[:, :].bitcast(I32), 1, None,
                                            ALU.logical_shift_right).then_inc(norm_step, 1)
                    dve.wait_ge(norm_step, done + GROUP + 3)
                    if has_before:
                        dve.wait_ge(feat_ready, (g - 1) * GROUP)
                    nc.vector.tensor_scalar(rstd[:, b, :].bitcast(I32), seed[:, :], -1.0, RSQRT_SEED,
                                            ALU.mult, ALU.add).then_inc(norm_step, 1)
                    return
                n = done + GROUP + 4 + 3 * (part - 1)
                dve.wait_ge(norm_step, n)
                nc.vector.tensor_tensor(newton[:, :], rstd[:, b, :], rstd[:, b, :], ALU.mult) \
                    .then_inc(norm_step, 1)
                dve.wait_ge(norm_step, n + 1)
                nc.vector.scalar_tensor_tensor(out=newton[:, :], in0=newton[:, :], scalar=-0.5,
                                               in1=var_eps[:, :], op0=ALU.mult, op1=ALU.mult) \
                    .then_inc(norm_step, 1)
                dve.wait_ge(norm_step, n + 2)
                nc.vector.scalar_tensor_tensor(out=rstd[:, b, :], in0=newton[:, :], scalar=1.5,
                                               in1=rstd[:, b, :], op0=ALU.add, op1=ALU.mult) \
                    .then_inc(norm_step, 1)
                if part == NEWTON_STEPS:
                    dve.wait_ge(norm_step, n + 3)
                    nc.vector.scalar_tensor_tensor(out=shift[:, b, :], in0=mean_var[:, :, 0], scalar=-1.0,
                                                   in1=rstd[:, b, :], op0=ALU.mult, op1=ALU.mult) \
                        .then_inc(norm_ready, 1)

            def keep_scores(g, b):
                dve.wait_ge(h_ready, (g + 1) * GROUP)
                nc.vector.tensor_copy(s_all[:, :, bass.ts(g, GROUP)],
                                      h_buf[:, b, :, O:O + 2].rearrange("p t s -> p s t")) \
                    .then_inc(value_step, 1)

            def keep_d(g, b):
                done = g * VALUE_STEPS
                dve.wait_ge(d_ready, g + 1)
                nc.vector.tensor_scalar(d_scaled[:, b, :], d_col[:, b, :], VALUE_SCALE, None, ALU.mult) \
                    .then_inc(value_step, 1)
                dve.wait_ge(value_step, done + 2)
                nc.vector.tensor_copy(value_hi[:, bass.ts(g, GROUP), O], d_scaled[:, b, :]) \
                    .then_inc(value_step, 1)
                dve.wait_ge(value_step, done + 3)
                nc.vector.tensor_tensor(value_hi[:, bass.ts(g, GROUP), O + 1], d_scaled[:, b, :],
                                        value_hi[:, bass.ts(g, GROUP), O], ALU.subtract) \
                    .then_inc(value_step, 1)

            def two_groups(k, first, last):
                for b in range(2):
                    g = 2 * k + b
                    start = first and b == 0
                    ahead = not (last and b == 1)
                    for i in range(GROUP):
                        n = g * GROUP + i
                        dve.wait_ge(featT_done, n + 1)
                        if not (start and i < RING):
                            dve.wait_ge(h_done, n - RING + 1)
                        if start and i == RING - 1:
                            dve.wait_ge(norms_done, 1)
                            nc.vector.tensor_reduce(ext[:, 3:4], ps_norm, op=ALU.max, axis=AX.X) \
                                .then_inc(norms_read, 1)
                            nc.vector.tensor_reduce(ext[:, 4:5], ps_norm, op=ALU.min, axis=AX.X) \
                                .then_inc(norms_read, 1)
                        nc.vector.tensor_copy(featT[:, i % RING, :], ps_feat[i % RING]) \
                            .then_inc(featT_ready, 1)
                        if i < 4 and ahead:
                            measure(g + 1, 1 - b, k + b, 2 * i)
                            measure(g + 1, 1 - b, k + b, 2 * i + 1)
                        if 4 <= i <= 4 + NEWTON_STEPS and ahead:
                            normalise(g + 1, 1 - b, i - 4, not start)
                        if i == 3 and not start:
                            keep_scores(g - 1, 1 - b)
                            keep_d(g - 1, 1 - b)

            dve.wait_ge(x_first, 16)
            for i in range(GROUP):
                if i == ROWS:
                    dve.wait_ge(x_loaded[0], 16)
                nc.vector.bn_stats(stats[:, i, :], x_in[:, i, :]).then_inc(norm_step, 1)
            for part in range(NEWTON_STEPS + 1):
                normalise(0, 0, part, False)
            dve.wait_ge(w_loaded, 16 * (KC + 1))
            n = 0
            for k in range(KC):
                for a in range(2):
                    if n:
                        dve.wait_ge(wa_step, n)
                    nc.vector.scalar_tensor_tensor(out=scratch[:, :], in0=w_ext[:, k, 0:O], scalar=1.0,
                                                   in1=attn_bc[:, a, :], op0=ALU.mult, op1=ALU.mult,
                                                   accum_out=w_ext[:, k, O + a:O + a + 1]) \
                        .then_inc(wa_step, 1)
                    n += 1
            rounds(dve, GROUPS // 2, two_groups)

            nc.vector.tensor_tensor(s1_diag, ident[:, :].unsqueeze(1).to_broadcast([PART, ROWS, PART]),
                                    s_all[:, 0, 0:ROWS].unsqueeze(2).to_broadcast([PART, ROWS, PART]),
                                    ALU.mult).then_inc(s1_diag_ready, 1)
            keep_scores(GROUPS - 1, 1)
            dve.wait_ge(value_step, (GROUPS - 1) * VALUE_STEPS + 1)
            nc.vector.tensor_reduce(ext[:, 0:1], s_all[:, 1, :], op=ALU.max, axis=AX.X).then_inc(top_ready, 1)
            nc.vector.tensor_reduce(ext[:, 1:2], s_all[:, 1, :], op=ALU.min, axis=AX.X).then_inc(ext_step, 1)
            nc.vector.tensor_reduce(ext[:, 2:3], s_all[:, 0, :], op=ALU.min, axis=AX.X).then_inc(ext_step, 1)
            dve.wait_ge(topT_done, 1)
            nc.vector.tensor_reduce(top[:, :], ps_top[0:1, 0:PART], op=ALU.max, axis=AX.X) \
                .then_inc(top_row_ready, 1)
            dve.wait_ge(norms_read, 2)
            nc.vector.tensor_scalar(ext[:, 4:5], ext[:, 4:5], -1.0, None, ALU.mult).then_inc(ext_step, 1)
            dve.wait_ge(ext_step, 3)
            nc.vector.tensor_scalar(ext[:, 1:3], ext[:, 1:3], -1.0, None, ALU.mult).then_inc(ext_ready, 1)
            dve.wait_ge(top_done, 1)
            nc.vector.tensor_scalar(ur_bias[:, :], ps_top[:, PART:PART + 1], SLOPE - 1.0,
                                    math.log(WEIGHT_SCALE), ALU.mult, ALU.add).then_inc(bias_ready, 1)

            def spread_extremes():
                dve.wait_ge(extT_done, 1)
                nc.vector.tensor_reduce(row_max[:, :], ps_ext[0:EXT, 0:PART], op=ALU.max, axis=AX.X) \
                    .then_inc(ext_step, 1)
                dve.wait_ge(ext_step, 4)
                nc.vector.tensor_scalar(row_diag[:, :], ident[0:EXT, 0:EXT], row_max[:, 0:1], None, ALU.mult) \
                    .then_inc(diag_ready, 1)
                dve.wait_ge(glob_done, 1)
                nc.vector.tensor_copy(glob[:, :], ps_ext[:, PART:PART + EXT]).then_inc(glob_read, 1)

            def find_limits():
                dve.wait_ge(glob_read, 1)
                for i, limit in ((0, S2_LIMIT), (1, S2_LIMIT), (3, NORM_LIMIT), (4, -NORM_LEAST)):
                    nc.vector.tensor_scalar(kept[:, i:i + 1], glob[:, i:i + 1], limit, None, ALU.is_le) \
                        .then_inc(over_step, 1)
                for i, a, b, op in ((2, 2, 0, ALU.subtract), (5, 1, 0, ALU.add)):
                    nc.vector.tensor_tensor(kept[:, i:i + 1], glob[:, a:a + 1], glob[:, b:b + 1], op) \
                        .then_inc(over_step, 1)
                dve.wait_ge(over_step, 6)
                for i, limit in ((2, S1_LIMIT), (5, SPREAD_LIMIT)):
                    nc.vector.tensor_scalar(kept[:, i:i + 1], kept[:, i:i + 1], limit, None, ALU.is_le) \
                        .then_inc(over_step, 1)
                dve.wait_ge(over_step, 8)
                nc.vector.tensor_reduce(within[:, :], kept[:, :], op=ALU.min, axis=AX.X) \
                    .then_inc(over_step, 1)

            def decide():
                dve.wait_ge(least_ready, QUADS + 1)
                nc.vector.tensor_reduce(den[:, 0, 0:1], least_den[:, :], op=ALU.min, axis=AX.X) \
                    .then_inc(over_step, 1)
                dve.wait_ge(over_step, 10)
                nc.vector.tensor_scalar(den[:, 0, 1:2], den[:, 0, 0:1], 0.0, None, ALU.is_gt) \
                    .then_inc(over_step, 1)
                dve.wait_ge(over_step, 11)
                nc.vector.tensor_scalar(all_within[:, :], den[:, 0, 1:2], within[:, 0:1], None, ALU.mult) \
                    .then_inc(within_ready, 1)
                dve.wait_ge(within_summed, 1)
                nc.vector.tensor_scalar(over_any[:, :], ps_within, float(PART), None, ALU.is_lt) \
                    .then_inc(over_ready, 1)

            def weigh(q, c, start):
                s = STAGES * q + c
                if c == 0:
                    if not start:
                        dve.wait_ge(r_loaded, 16 * q)
                        dve.wait_ge(p_ready, s)
                        nc.vector.tensor_copy(r_bc[:, :], r_in[:, :]).then_inc(r_ready, 1)
                    dve.wait_ge(r_ready, q + 1)
                dve.wait_ge(pT_done, s + 1)
                if not (start and c < RING):
                    dve.wait_ge(lo_ready, s - RING + 1)
                dve.nop(nofuse=True)
                for j in range(BLOCKS):
                    part = slice(j * WIDE, (j + 1) * WIDE)
                    last = nc.vector.scalar_tensor_tensor(
                        out=pT[c % RING][:, part], in0=r_bc[:, :], scalar=u_col[:, c * BLOCKS + j:c * BLOCKS + j + 1],
                        in1=ps_mask[c % RING][:, j, :], op0=ALU.max, op1=ALU.mult)
                last.then_inc(p_ready, 1)

            def cut_p(q, c):
                dve.wait_ge(hi_ready, STAGES * q + c + 1)
                nc.vector.scalar_tensor_tensor(out=pT_lo[:, c % RING, :], in0=pT[c % RING],
                                               scalar=0.0, in1=pT_hi[:, c % RING, :],
                                               op0=ALU.max, op1=ALU.subtract).then_inc(lo_ready, 1)

            def denominators(q):
                for r in range(ROWS):
                    dve.wait_ge(acc_copied[r], q + 1)
                nc.vector.tensor_tensor(den[:, 0, :], acc_sb[:, :, O], acc_sb[:, :, O + 1], ALU.add) \
                    .then_inc(den_ready, 1)
                dve.wait_ge(den_ready, q + 1)
                nc.vector.reciprocal(den[:, 1, :], den[:, 0, :]).then_inc(rden_ready, 1)
                dve.wait_ge(least_ready, q + 1)
                nc.vector.tensor_tensor(least_den[:, :], least_den[:, :], den[:, 0, :], ALU.min) \
                    .then_inc(least_ready, 1)

            def quad(q, first, last):
                for c in range(STAGES):
                    if c + LEAD < STAGES:
                        weigh(q, c + LEAD, first)
                    elif not last:
                        weigh(q + 1, c + LEAD - STAGES, False)
                    cut_p(q, c)
                    if not first:
                        if c == 3:
                            denominators(q - 1)

            dve.wait_ge(u_ready, 1)
            dve.wait_ge(h_stored[0], 16 * (GROUPS // 2))
            dve.wait_ge(scaled_ready, GROUPS - 1)
            weigh(0, 0, True)
            spread_extremes()
            for c in range(1, LEAD):
                weigh(0, c, True)
            keep_d(GROUPS - 1, 1)
            find_limits()
            rounds(dve, QUADS, quad)
            denominators(QUADS - 1)
            decide()
            dve.wait_ge(y_ready, QUADS)
            dve.wait_ge(x_back, 16 * QUADS)
            dve.wait_ge(out_ready, QUADS - 1)
            nc.vector.scalar_tensor_tensor(out=x_plus, in0=y, scalar=0.0, in1=x_quad[:, :],
                                           op0=ALU.max, op1=ALU.add).then_inc(xp_ready, 1)
            dve.wait_ge(xp_ready, QUADS)
            dve.wait_ge(expm_ready, QUADS)
            dve.wait_ge(out_stored, 16 * QUADS)
            nc.vector.scalar_tensor_tensor(out=out_quad[:, :], in0=expm, scalar=-1.0, in1=x_plus,
                                           op0=ALU.add, op1=ALU.add).then_inc(out_ready, 1)

            def general():
                STEPS = 3 * CHUNKS + 1

                def scores(t, c):
                    done = t * STEPS + 3 * c + 1
                    dve.wait_ge(g_step, done)
                    dve.wait_ge(g_adj_loaded, 16 * CHUNKS * t + 16 * c + 16)
                    nc.vector.tensor_scalar(edge.rearrange("p (m k n) -> p m k n", k=ROWS, n=PART),
                                            g_adj.rearrange("p (m n k) -> p m k n", k=ROWS, n=PART),
                                            0.0, 0.5, ALU.is_gt, ALU.subtract).then_inc(g_adj_read, 1)
                    part = slice(c * CHUNK, (c + 1) * CHUNK)
                    nc.vector.tensor_scalar(raw, s2_bc[:, part], s1_cur[:, 0:1], None, ALU.add) \
                        .then_inc(g_step, 1)
                    dve.wait_ge(g_step, done + 1)
                    nc.vector.scalar_tensor_tensor(out=leaky, in0=raw, scalar=SLOPE, in1=raw,
                                                   op0=ALU.mult, op1=ALU.max).then_inc(g_step, 1)
                    dve.wait_ge(g_step, done + 2)
                    dve.wait_ge(g_adj_read, CHUNKS * t + c + 1)
                    nc.vector.scalar_tensor_tensor(out=score[:, part], in0=edge, scalar=2 * MASKED,
                                                   in1=leaky, op0=ALU.mult, op1=ALU.min) \
                        .then_inc(g_step, 1)

                dve.wait_ge(g_s2T_done, 1)
                nc.vector.tensor_copy(s2T[:, :], ring[0][0:TILES, 0:PART]).then_inc(g_s2T_ready, 1)
                dve.wait_ge(g_s2_loaded, 16)
                with dve.Fori(0, TILES) as t:
                    nc.vector.tensor_copy(s1_cur[:, :], s_all[:, 0, bass.ds(t, 1)]).then_inc(g_step, 1)
                    for c in range(CHUNKS):
                        scores(t, c)
                    dve.wait_ge(g_step, t * STEPS + STEPS)
                    nc.vector.tensor_reduce(neg_max[:, 0:1], score, op=ALU.max, axis=AX.X) \
                        .then_inc(g_top_ready, 1)
                    dve.wait_ge(g_top_ready, t + 1)
                    nc.vector.tensor_scalar(neg_max[:, 1:2], neg_max[:, 0:1], -1.0, None, ALU.mult) \
                        .then_inc(g_max_ready, 1)
                    for n in range(FOUR):
                        dve.wait_ge(g_wT_done, FOUR * t + n + 1)
                        if n >= 2:
                            dve.wait_ge(g_summed, FOUR * t + n - 1)
                        nc.vector.tensor_copy(wT[:, n % 2, :], ring[n % 2][:, :]).then_inc(g_wT_ready, 1)
                    dve.wait_ge(g_w_ready, t + 1)
                    nc.vector.reciprocal(g_den[:, 1:2], g_den[:, 0:1]).then_inc(g_rden_ready, 1)
                    dve.wait_ge(g_rden_ready, t + 1)
                    dve.wait_ge(g_summed, FOUR * t + FOUR)
                    nc.vector.tensor_scalar(g_y[:, 0:O], acc[0][:, 0:O], g_den[:, 1:2], None,
                                            ALU.mult).then_inc(g_y_ready, 1)
                    dve.wait_ge(g_y_ready, t + 1)
                    dve.wait_ge(g_x_loaded, 16 * t + 16)
                    nc.vector.scalar_tensor_tensor(out=x_quad[:, F:2 * F], in0=g_y[:, 0:O],
                                                   scalar=0.0, in1=x_quad[:, 0:F],
                                                   op0=ALU.max, op1=ALU.add).then_inc(g_xp_ready, 1)
                    dve.wait_ge(g_xp_ready, t + 1)
                    dve.wait_ge(g_expm_ready, t + 1)
                    nc.vector.scalar_tensor_tensor(out=out_quad[:, 0:O], in0=neg_part[:, O:2 * O],
                                                   scalar=-1.0, in1=x_quad[:, F:2 * F],
                                                   op0=ALU.add, op1=ALU.add).then_inc(g_out_ready, 1)
                    dve.wait_ge(g_out_ready, t + 1)

            in_general(dve, general)

        @block.tensor
        def _(pe):
            def transpose_feat(g, i, start):
                n = g * GROUP + i
                pe.wait_ge(feat_ready, n + 1)
                if not (start and i < RING):
                    pe.wait_ge(featT_ready, n - RING + 1)
                for k in range(KC):
                    last = nc.tensor.transpose(ps_feat[i % RING][:, k * PART:(k + 1) * PART],
                                               feat[:, i % RING, k * PART:(k + 1) * PART], ident[:, :])
                last.then_inc(featT_done, 1)

            def h_product(g, i, start):
                n = g * GROUP + i
                pe.wait_ge(featT_ready, n + 1)
                if not (start and i < RING):
                    pe.wait_ge(h_ready, n - RING + 1)
                for k in range(KC):
                    last = nc.tensor.matmul(ps_h[i % RING], featT[:, i % RING, k * PART:(k + 1) * PART],
                                            w_ext[:, k, :], start=(k == 0), stop=(k == KC - 1))
                last.then_inc(h_done, 1)

            def two_groups(k, first, last):
                for b in range(2):
                    g = 2 * k + b
                    start = first and b == 0
                    for i in range(GROUP):
                        transpose_feat(g, i, start)
                        if start and i == 1:
                            pe.wait_ge(wa_step, 2 * KC)
                        if i > 0:
                            h_product(g, i - 1, start)
                        elif not start:
                            h_product(g - 1, GROUP - 1, False)
                    if last and b == 1:
                        h_product(g, GROUP - 1, False)

            pe.wait_ge(const_ready, 4)
            pe.wait_ge(w_sq_ready, 1)
            for k in range(KC):
                last = nc.tensor.matmul(ps_norm, ones[:, :], w_sq[:, k, :], start=(k == 0), stop=(k == KC - 1))
            last.then_inc(norms_done, 1)
            rounds(pe, GROUPS // 2, two_groups)

            def transpose_mask(q, c, start):
                s = STAGES * q + c
                if c % PER_PIECE == 0:
                    pe.wait_ge(mask_ready, 2 * (PIECES * q + c // PER_PIECE + 1))
                if not (start and c < RING):
                    pe.wait_ge(p_ready, s - RING + 1)
                for r in range(ROWS):
                    last = nc.tensor.transpose(ps_pairs[c % RING][:, r * PART:(r + 1) * PART],
                                               mask_pairs[:, c // PER_PIECE % RING, r, c % PER_PIECE, :],
                                               ident_bf[:, :])
                last.then_inc(pT_done, 1)

            def add_hi(c, j, r):
                node = c * BLOCKS + j
                w = pT_hi[:, c % RING, j * WIDE + r * PART:j * WIDE + (r + 1) * PART]
                nc.tensor.matmul(acc[r][:, 0:O + 2], w, value_hi[:, node, :], start=(node == 0), stop=False)
                nc.tensor.matmul(acc[r][:, 0:O], w, value_lo[:, node, :], start=False, stop=False)

            def add_lo(c, j, r):
                node = c * BLOCKS + j
                w = pT_lo[:, c % RING, j * WIDE + r * PART:j * WIDE + (r + 1) * PART]
                return nc.tensor.matmul(acc[r][:, 0:O + 1], w, value_hi[:, node, 0:O + 1],
                                        start=False, stop=(node == TILES - 1))

            def quad(q, first, last):
                for c in range(STAGES):
                    s = STAGES * q + c
                    pe.wait_ge(hi_ready, s + 1)
                    if first and c * BLOCKS % GROUP == 0:
                        pe.wait_ge(lo_cut, c * BLOCKS // GROUP + 1)
                    if c < STAGES - 1:
                        for r in range(ROWS):
                            if c == 0 and not first:
                                pe.wait_ge(acc_copied[r], q)
                            for j in range(BLOCKS):
                                add_hi(c, j, r)
                    if c + AHEAD < STAGES:
                        transpose_mask(q, c + AHEAD, first)
                    elif not last:
                        transpose_mask(q + 1, c + AHEAD - STAGES, False)
                    pe.wait_ge(lo_ready, s + 1)
                    if c < STAGES - 1:
                        for r in range(ROWS):
                            for j in range(BLOCKS):
                                end = add_lo(c, j, r)
                        end.then_inc(stage_summed, 1)
                    else:
                        for r in range(ROWS):
                            for j in range(BLOCKS):
                                add_hi(c, j, r)
                            for j in range(BLOCKS):
                                end = add_lo(c, j, r)
                            end.then_inc(row_summed if r < ROWS - 1 else stage_summed, 1)

            pe.wait_ge(h_ready, TILES)
            pe.wait_ge(s1_diag_ready, 1)
            nc.tensor.matmul(ps_s1[:, 0:WIDE], ones[:, :], r_in[:, :], start=True, stop=True).then_inc(s1_done, 1)
            pe.wait_ge(top_ready, 1)
            nc.tensor.transpose(ps_top[0:1, 0:PART], ext[:, 0:1], ident[:, :]).then_inc(topT_done, 1)
            pe.wait_ge(top_row_ready, 1)
            nc.tensor.matmul(ps_top[:, PART:PART + 1], ones[0:1, :], top[:, :], start=True, stop=True) \
                .then_inc(top_done, 1)
            nc.tensor.transpose(ps_s[0:TILES, 0:PART], s_all[:, 0, :], ident[:, :]).then_inc(sT_done, 1)
            for c in range(PER_PIECE):
                transpose_mask(0, c, True)
            pe.wait_ge(ext_ready, 1)
            nc.tensor.transpose(ps_ext[0:EXT, 0:PART], ext[:, :], ident[:, :]).then_inc(extT_done, 1)
            pe.wait_ge(diag_ready, 1)
            nc.tensor.matmul(ps_ext[:, PART:PART + EXT], ones[0:EXT, :], row_diag[:, :],
                             start=True, stop=True).then_inc(glob_done, 1)
            for c in range(PER_PIECE, AHEAD):
                transpose_mask(0, c, True)
            pe.wait_ge(rT_ready, 1)
            pe.wait_ge(glob_read, 1)
            rounds(pe, QUADS, quad)

            pe.wait_ge(p_ready, QUADS * STAGES)
            pe.wait_ge(within_ready, 1)
            nc.tensor.matmul(ps_within, ones[:, :], all_within[:, :], start=True, stop=True) \
                .then_inc(within_summed, 1)

            def general():
                pe.wait_ge(g_h_loaded, 16)
                nc.tensor.transpose(ring[0][0:TILES, 0:PART], s_all[:, 1, :], ident[:, :]) \
                    .then_inc(g_s2T_done, 1)

                def transpose_w(t, n):
                    if n >= 2:
                        pe.wait_ge(g_wT_ready, FOUR * t + n - 1)
                    for j in range(4):
                        at = (4 * n + j) * PART
                        last = nc.tensor.transpose(ring[n % 2][:, j * PART:(j + 1) * PART],
                                                   score[:, at:at + PART], ident[:, :])
                    last.then_inc(g_wT_done, 1)

                with pe.Fori(0, TILES) as t:
                    pe.wait_ge(g_w_ready, t + 1)
                    transpose_w(t, 0)
                    for n in range(FOUR):
                        if n + 1 < FOUR:
                            transpose_w(t, n + 1)
                        pe.wait_ge(g_wT_ready, FOUR * t + n + 1)
                        for j in range(4):
                            node = 4 * n + j
                            last = nc.tensor.matmul(acc[0][:, 0:O], wT[:, n % 2, j * PART:(j + 1) * PART],
                                                    h_all[:, node, :], start=(node == 0),
                                                    stop=(node == TILES - 1))
                        last.then_inc(g_summed, 1)

            in_general(pe, general)


_INS = ['x', 'adj', 'L0_gnn_W', 'L0_gnn_attn']


def kernel(**inputs):
    import numpy as _np
    import concourse.bacc as _bacc
    from concourse import mybir as _mybir
    from concourse.bass_utils import run_bass_kernel_spmd as _run

    nc = _bacc.Bacc("TRN2", target_bir_lowering=False, num_devices=1)
    arrays, args = {}, []
    for name in _INS:
        a = _np.ascontiguousarray(inputs[name])
        arrays[f"in_{name}_dram"] = a
        args.append(nc.dram_tensor(f"in_{name}_dram", a.shape, _mybir.dt.from_np(a.dtype), kind="ExternalInput").ap())
    x = arrays["in_x_dram"]
    args.append(nc.dram_tensor("out_dram", x.shape, _mybir.dt.from_np(x.dtype), kind="ExternalOutput").ap())
    gat_kernel(nc, *args)
    r = _run(nc, [arrays], core_ids=[0])
    return r.results[0]["out_dram"]
```
